# Optimizing a Trainium2 kernel written in Bass

```python
import numpy as np
import jax
import jax.numpy as jnp

def _softmax(x, axis=-1):
    return jax.nn.softmax(x, axis=axis)

def _gelu(x):
    return jax.nn.gelu(x, approximate=True)

def _silu(x):
    return jax.nn.silu(x)

def _sigmoid(x):
    return jax.nn.sigmoid(x)

def _layernorm(x, axis=-1, eps=1e-05):
    m = jnp.mean(x, axis=axis, keepdims=True)
    v = jnp.var(x, axis=axis, keepdims=True)
    return (x - m) / jnp.sqrt(v + eps)

def _scatter_add(tgt, idx, src, axis=0):
    return tgt.at[idx].add(src)

def _segment_sum(src, seg, n):
    return jax.ops.segment_sum(src, seg, n)
kernel_name = 'mk_macaron_d1_jaxref_r4_77af8a'

def setup_inputs(seed: int=0):
    np.random.seed(seed)
    _w = jnp.asarray

    def _L0_attn_setup():
        import jax, jax.numpy as jnp
        import numpy as np
        import math
        B, S, HID = (2, 1000, 256)
        H, W, STRIDE = (16, 128, 64)
        D = HID // H
        key = jax.random.key(seed)
        ks = jax.random.split(key, 10)
        std = 0.02
        inp = {'hidden_states': jax.random.normal(ks[0], (B, S, HID), dtype=jnp.float32), 'Wq': jax.random.normal(ks[1], (HID, HID), dtype=jnp.float32) * std, 'bq': jnp.zeros((HID,), dtype=jnp.float32), 'Wk': jax.random.normal(ks[2], (HID, HID), dtype=jnp.float32) * std, 'bk': jnp.zeros((HID,), dtype=jnp.float32), 'Wv': jax.random.normal(ks[3], (HID, HID), dtype=jnp.float32) * std, 'bv': jnp.zeros((HID,), dtype=jnp.float32), 'Wo': jax.random.normal(ks[4], (HID, HID), dtype=jnp.float32) * std, 'bo': jnp.zeros((HID,), dtype=jnp.float32), 'pos_bias': jax.random.normal(ks[5], (H, W, W), dtype=jnp.float32) * std}
        return inp
    _L0_attn_in = _L0_attn_setup()

    def _L0_ffn_setup():
        import jax, jax.numpy as jnp
        import numpy as np
        D_MODEL = 256
        FFN_DIM = 512
        NUM_EXPERTS = 8
        NUM_GROUPS = 4
        EXPERTS_PER_GROUP = NUM_EXPERTS // NUM_GROUPS
        TOP_K = 2
        GROUPS_TOP_K = 1
        EPS = 1e-09

        def _topk_normalized(scores, k):
            vals, idx = jax.lax.top_k(scores, k)
            vals = vals / (jnp.sum(vals, axis=-1, keepdims=True) + EPS)
            return (vals, idx)
        key = jax.random.key(seed)
        ks = jax.random.split(key, 6)
        B, S = (2, 256)
        x = jax.random.normal(ks[0], (B, S, D_MODEL), dtype=jnp.float32)
        sd = 0.02
        macro_w = jax.random.normal(ks[1], (D_MODEL, NUM_GROUPS), dtype=jnp.float32) * sd
        micro_w = jax.random.normal(ks[2], (NUM_GROUPS, D_MODEL, EXPERTS_PER_GROUP), dtype=jnp.float32) * sd
        gate_w = jax.random.normal(ks[3], (NUM_EXPERTS, D_MODEL, FFN_DIM), dtype=jnp.float32) * sd
        up_w = jax.random.normal(ks[4], (NUM_EXPERTS, D_MODEL, FFN_DIM), dtype=jnp.float32) * sd
        down_w = jax.random.normal(ks[5], (NUM_EXPERTS, FFN_DIM, D_MODEL), dtype=jnp.float32) * sd
        return {'x': x, 'macro_w': macro_w, 'micro_w': micro_w, 'gate_w': gate_w, 'up_w': up_w, 'down_w': down_w}
    _L0_ffn_in = _L0_ffn_setup()
    _d = {'L0_attn_hidden_states': _L0_attn_in['hidden_states'], 'L0_attn_Wq': _L0_attn_in['Wq'], 'L0_attn_bq': _L0_attn_in['bq'], 'L0_attn_Wk': _L0_attn_in['Wk'], 'L0_attn_bk': _L0_attn_in['bk'], 'L0_attn_Wv': _L0_attn_in['Wv'], 'L0_attn_bv': _L0_attn_in['bv'], 'L0_attn_Wo': _L0_attn_in['Wo'], 'L0_attn_bo': _L0_attn_in['bo'], 'L0_attn_pos_bias': _L0_attn_in['pos_bias'], 'L0_ffn_macro_w': _L0_ffn_in['macro_w'], 'L0_ffn_micro_w': _L0_ffn_in['micro_w'], 'L0_ffn_gate_w': _L0_ffn_in['gate_w'], 'L0_ffn_up_w': _L0_ffn_in['up_w'], 'L0_ffn_down_w': _L0_ffn_in['down_w']}
    _x0 = _d['L0_attn_hidden_states']
    _d['L0_attn_hidden_states'] = jax.random.normal(jax.random.fold_in(jax.random.key(seed), 1), (8, 512, 256), dtype=_x0.dtype)
    del _x0
    return _d

def reference(L0_attn_hidden_states, L0_attn_Wq, L0_attn_bq, L0_attn_Wk, L0_attn_bk, L0_attn_Wv, L0_attn_bv, L0_attn_Wo, L0_attn_bo, L0_attn_pos_bias, L0_ffn_macro_w, L0_ffn_micro_w, L0_ffn_gate_w, L0_ffn_up_w, L0_ffn_down_w):

    def _L0_attn_ref(hidden_states, Wq, bq, Wk, bk, Wv, bv, Wo, bo, pos_bias):
        import jax, jax.numpy as jnp
        import numpy as np
        import math
        B, S, HID = (2, 1000, 256)
        H, W, STRIDE = (16, 128, 64)
        D = HID // H
        Bb, Ss, Hid = hidden_states.shape
        scale = 1.0 / math.sqrt(D)

        def split_heads(x):
            return x.reshape(Bb, Ss, H, D).transpose(0, 2, 1, 3)
        q = split_heads(hidden_states @ Wq + bq)
        k = split_heads(hidden_states @ Wk + bk)
        v = split_heads(hidden_states @ Wv + bv)
        n_win = (Ss - W) // STRIDE + 1
        starts = jnp.arange(n_win) * STRIDE
        idx = starts[:, None] + jnp.arange(W)
        qw = q[:, :, idx]
        kw = k[:, :, idx]
        vw = v[:, :, idx]
        scores = jnp.einsum('bhnqd,bhnkd->bhnqk', qw, kw) * scale + pos_bias[None, :, None]
        probs = jax.nn.softmax(scores, axis=-1)
        ow = jnp.einsum('bhnqk,bhnkd->bhnqd', probs, vw)
        flat = idx.reshape(-1)
        merged = jnp.zeros((Bb, H, Ss, D), dtype=ow.dtype).at[:, :, flat].add(ow.reshape(Bb, H, -1, D))
        counts = jnp.zeros((Ss,), dtype=jnp.float32).at[flat].add(1.0)
        ls = Ss - W
        qt, kt, vt = (q[:, :, ls:], k[:, :, ls:], v[:, :, ls:])
        st = jnp.einsum('bhqd,bhkd->bhqk', qt, kt) * scale + pos_bias[None]
        ot = jnp.einsum('bhqk,bhkd->bhqd', jax.nn.softmax(st, axis=-1), vt)
        merged = merged.at[:, :, ls:].add(ot)
        counts = counts.at[ls:].add(1.0)
        merged = merged / jnp.clip(counts, 1.0, None)[None, None, :, None]
        ctx = merged.transpose(0, 2, 1, 3).reshape(Bb, Ss, Hid)
        return ctx @ Wo + bo

    def _L0_ffn_ref(x, macro_w, micro_w, gate_w, up_w, down_w):
        import jax, jax.numpy as jnp
        import numpy as np
        D_MODEL = 256
        FFN_DIM = 512
        NUM_EXPERTS = 8
        NUM_GROUPS = 4
        EXPERTS_PER_GROUP = NUM_EXPERTS // NUM_GROUPS
        TOP_K = 2
        GROUPS_TOP_K = 1
        EPS = 1e-09

        def _topk_normalized(scores, k):
            vals, idx = jax.lax.top_k(scores, k)
            vals = vals / (jnp.sum(vals, axis=-1, keepdims=True) + EPS)
            return (vals, idx)
        B, S, D = x.shape
        T = B * S
        xf = x.reshape(T, D)
        macro_scores = jax.nn.sigmoid(xf @ macro_w)
        mv, mi = _topk_normalized(macro_scores, GROUPS_TOP_K)
        macro_full = jnp.sum(jax.nn.one_hot(mi, NUM_GROUPS, dtype=xf.dtype) * mv[..., None], axis=1)
        micro_scores = jax.nn.sigmoid(jnp.einsum('td,gde->tge', xf, micro_w))
        uv, ui = _topk_normalized(micro_scores, TOP_K)
        micro_full = jnp.sum(jax.nn.one_hot(ui, EXPERTS_PER_GROUP, dtype=xf.dtype) * uv[..., None], axis=2)
        w = (macro_full[:, :, None] * micro_full).reshape(T, NUM_EXPERTS)
        gate = jax.nn.silu(jnp.einsum('td,edf->tef', xf, gate_w))
        up = jnp.einsum('td,edf->tef', xf, up_w)
        h = gate * up
        out = jnp.einsum('te,tef,efd->td', w, h, down_w)
        return out.reshape(B, S, D)
    x = L0_attn_hidden_states
    x = x + 0.5 * _L0_ffn_ref(_layernorm(x, axis=-1), L0_ffn_macro_w, L0_ffn_micro_w, L0_ffn_gate_w, L0_ffn_up_w, L0_ffn_down_w)
    x = x + _L0_attn_ref(_layernorm(x, axis=-1), L0_attn_Wq, L0_attn_bq, L0_attn_Wk, L0_attn_bk, L0_attn_Wv, L0_attn_bv, L0_attn_Wo, L0_attn_bo, L0_attn_pos_bias)
    x = x + 0.5 * _L0_ffn_ref(_layernorm(x, axis=-1), L0_ffn_macro_w, L0_ffn_micro_w, L0_ffn_gate_w, L0_ffn_up_w, L0_ffn_down_w)
    return x

_drawn_inputs = setup_inputs


def setup_inputs(seed=0):
    import zlib

    import numpy as np

    out = dict(_drawn_inputs(seed))
    spreads = {'L0_attn_bq': (0.0, 0.8),
     'L0_attn_bk': (0.0, 0.8),
     'L0_attn_bv': (0.0, 0.1),
     'L0_attn_bo': (0.0, 0.1)}
    factors = {'L0_attn_Wq': 8.0,
     'L0_attn_Wk': 8.0,
     'L0_attn_Wv': 6.928,
     'L0_attn_pos_bias': 8.0,
     'L0_ffn_macro_w': 3.918,
     'L0_ffn_micro_w': 8.0,
     'L0_ffn_gate_w': 3.431,
     'L0_ffn_up_w': 3.39,
     'L0_ffn_down_w': 3.387}
    for name, (base, spread) in spreads.items():
        noise = np.random.default_rng([zlib.crc32(name.encode()), seed]).standard_normal(out[name].shape)
        drawn = base * np.exp(spread * noise) if base else spread * noise
        out[name] = jnp.asarray(drawn.astype(out[name].dtype))
    for name, factor in factors.items():
        out[name] = (out[name] * factor).astype(out[name].dtype)
    return out
```

```python
import concourse.bass as bass
from concourse import mybir
from contextlib import ExitStack

F32 = mybir.dt.float32
I32 = mybir.dt.int32
ALU = mybir.AluOpType
ACT = mybir.ActivationFunctionType
AX = mybir.AxisListType

P = 128
B, S, D = 8, 512, 256
T = B * S
NT = T // P
TB = S // P
DC = D // P
F = 512
FC = F // P
G, E = 4, 2
NEXP = G * E
NS = NT + G - 1
NR = G + NEXP
RW = D + E
H, HD = 16, 16
W, STRIDE = 128, 64
NWIN = (S - W) // STRIDE + 1
HQ = 4
NQ = H // HQ
UNITS = NWIN * NQ
HS = 32
HC = P // HD
LN_EPS = 1e-5
TOPK_EPS = 1e-9
BIG = 3.0e38
OPEN = 1


def macaron_kernel(nc, x_in, Wq, bq, Wk, bk, Wv, bv, Wo, bo, pos_bias, macro_w, micro_w, gate_w, up_w, down_w, out):
    ctx = ExitStack()
    with ctx:
        def sb(name, shape, dt=F32):
            return ctx.enter_context(nc.sbuf_tensor(name, shape, dt))

        def sem(name):
            return ctx.enter_context(nc.semaphore(name))

        sorted_rows = nc.dram_tensor("sorted_rows", [NS * P, RW], F32, kind="Internal").ap()
        sorted_out = nc.dram_tensor("sorted_out", [NS * P, D], F32, kind="Internal").ap()

        res = sb("res", [P, NT, D])
        wgu = sb("wgu", [P, 2 * DC * NEXP * F])
        wd = sb("wd", [P, FC, NEXP, D])
        wg = wgu[:, 0:DC * NEXP * F].rearrange("p (c e f) -> p c e f", c=DC, e=NEXP)
        wu = wgu[:, DC * NEXP * F:].rearrange("p (c e f) -> p c e f", c=DC, e=NEXP)
        big = sb("big", [P, NS * RW])
        rows = big[:, :].rearrange("p (t r) -> p t r", r=RW)

        ident = sb("ident", [P, P])
        tri = sb("tri", [P, P])
        ones = sb("ones", [P, P])
        wr = sb("wr", [P, DC, NR])
        stats = sb("stats", [P, NT, 6])
        mean = sb("mean", [P, NT])
        rstd = sb("rstd", [P, NT])
        ln_t = sb("ln_t", [P, 4, NT])
        xn2 = sb("xn2", [P, 2, D])
        xs = sb("xs", [P, RW])[:]
        wts = sb("wts", [P, NS, E])
        rt = sb("rt", [P, 2, DC, P])
        sg = sb("sg", [P, NT, NR])
        oh = sb("oh", [P, G, NT])
        rsc = sb("rsc", [P, 8, NT])
        cnt = sb("cnt", [P, G, NT])
        pre = sb("pre", [P, G, NT])
        gsc = sb("gsc", [P, 4, G])
        gint = sb("gint", [P, 2, G], I32)
        posf = sb("posf", [P, NT])
        pos = sb("pos", [P, NT], I32)
        tile_no = sb("tile_no", [P, NS])
        tgrp_f = sb("tgrp_f", [P, 2, NS])
        tile_group = sb("tile_group", [P, NS], I32)
        xt = sb("xt", [P, DC, P])
        sl = sb("sl", [P, E, F])
        hb = sb("hb", [P, E, F])
        ht = sb("ht", [P, E, F])

        at = [0]

        def part(*shape):
            n = 1
            for k in shape:
                n *= k
            v = wgu[:, at[0]:at[0] + n]
            at[0] += n
            names = "abcd"[:len(shape)]
            if len(shape) > 1:
                v = v.rearrange(f"p ({' '.join(names)}) -> p {' '.join(names)}",
                                **{c: k for c, k in zip(names, shape)})
            return v

        nbias = part(H, W)
        wq_s, wk_s, wv_s = part(DC, D), part(DC, D), part(DC, D)
        wo_s = part(NQ, D)
        bv_s = part(D)
        xa = part(TB, D)
        xnt = part(DC, S)
        qt = part(DC, S)
        kt = part(DC, S)
        va = part(NWIN, H, HS)
        sbuf_s = part(2, HQ, W)
        prob = part(2, HQ, W)
        pt_s = part(2, HQ * W)
        nmax = part(2, HQ)
        rcp = sb("rcp", [P, NQ, W])[:]
        ct = sb("ct", [P, 2, NQ, W])
        ctxt = sb("ctxt", [P, NQ, S])
        inv_count = sb("inv_count", [P, S])[:]
        qkb = part(4, DC)
        km = big[:, 0:H * S].rearrange("p (h s) -> p h s", h=H)

        bank = [ctx.enter_context(nc.psum_tensor(f"bank{i}", [P, 512], F32)) for i in range(8)]

        const_made = sem("const_made")
        zero_made = sem("zero_made")
        rows_zeroed = sem("rows_zeroed")
        x_loaded = sem("x_loaded")
        wr_loaded = sem("wr_loaded")
        w_loaded = sem("w_loaded")
        stats_done = sem("stats_done")
        dve_step = sem("dve_step")
        act_step = sem("act_step")
        var_ready = sem("var_ready")
        std_ready = sem("std_ready")
        xn_ready = sem("xn_ready")
        rt_psum = sem("rt_psum")
        rt_ready = sem("rt_ready")
        logits_done = sem("logits_done")
        sig_ready = sem("sig_ready")
        onehot_ready = sem("onehot_ready")
        rank_done = sem("rank_done")
        pos_ready = sem("pos_ready")
        scattered = sem("scattered")
        xs_loaded = sem("xs_loaded")
        xt_psum = sem("xt_psum")
        xt_ready = sem("xt_ready")
        gu_done = sem("gu_done")
        silu_done = sem("silu_done")
        h_ready = sem("h_ready")
        ht_psum = sem("ht_psum")
        ht0_ready = sem("ht0_ready")
        ht1_ready = sem("ht1_ready")
        d_done = sem("d_done")
        y_ready = sem("y_ready")
        y_stored = sem("y_stored")
        w_taken = sem("w_taken")
        x2_ready = sem("x2_ready")
        y_gathered = sem("y_gathered")
        res_ready = sem("res_ready")
        out_stored = sem("out_stored")
        aw_loaded = sem("aw_loaded")
        pads_made = sem("pads_made")
        acon_ready = sem("acon_ready")
        xa_ready = sem("xa_ready")
        xnt_psum = sem("xnt_psum")
        xnt0_ready = sem("xnt0_ready")
        xnt1_ready = sem("xnt1_ready")
        proj_done = sem("proj_done")
        q_ready = sem("q_ready")
        k_ready = sem("k_ready")
        v_ready = sem("v_ready")
        km_loaded = sem("km_loaded")
        s_done = sem("s_done")
        sb_ready = sem("sb_ready")
        p_ready = sem("p_ready")
        pt_psum = sem("pt_psum")
        pt_ready = sem("pt_ready")
        pv_done = sem("pv_done")
        rcp_ready = sem("rcp_ready")
        ct_ready = sem("ct_ready")
        acc_zero = sem("acc_zero")
        acc_done = sem("acc_done")
        ctx_ready = sem("ctx_ready")
        o_done = sem("o_done")
        res_attn = sem("res_attn")
        batch_open = sem("batch_open")
        unit_open = sem("unit_open")

        step = {"dve": 0}

        block = ctx.enter_context(nc.Block())

        @block.sync
        def _(sp):
            sp.sem_inc(km_loaded, OPEN)
            for b in range(B):
                sp.dma_start(res[:, b * TB:(b + 1) * TB, :],
                             x_in[b].rearrange("(t p) d -> p t d", p=P)).then_inc(x_loaded, 16)
            sp.dma_start(wr[:, :, 0:G], macro_w.rearrange("(c p) g -> p c g", p=P)).then_inc(wr_loaded, 16)
            for g in range(G):
                sp.dma_start(wr[:, :, G + E * g:G + E * g + E],
                             micro_w[g].rearrange("(c p) e -> p c e", p=P)).then_inc(wr_loaded, 16)
            sp.wait_ge(zero_made, 1)
            sp.dma_start(sorted_rows.rearrange("(t p) r -> p t r", p=P), rows).then_inc(rows_zeroed, 16)

            def load_gate_up():
                for e in range(NEXP):
                    sp.dma_start(wg[:, :, e, :], gate_w[e].rearrange("(c p) f -> p c f", p=P)).then_inc(w_loaded, 16)
                    sp.dma_start(wu[:, :, e, :], up_w[e].rearrange("(c p) f -> p c f", p=P)).then_inc(w_loaded, 16)

            load_gate_up()
            for e in range(NEXP):
                sp.dma_start(wd[:, :, e, :], down_w[e].rearrange("(c p) n -> p c n", p=P)).then_inc(w_loaded, 16)

            def ffn(n):
                t0 = n * NS
                sp.wait_ge(scattered, 16 * NT * (n + 1))
                with sp.Fori(0, NS) as j:
                    sp.wait_ge(xt_psum, j + t0 + OPEN)
                    sp.wait_ge(w_taken, j + t0 + OPEN)
                    sp.dma_start(xs, sorted_rows[bass.ds(j * P, P), :]).then_inc(xs_loaded, 16)

            ffn(0)
            sp.wait_ge(y_ready, NS + OPEN)
            sp.wait_ge(pads_made, 3)
            sp.dma_start(nbias, pos_bias.rearrange("h q k -> q h k")).then_inc(aw_loaded, 16)
            sp.dma_start(wq_s, Wq.rearrange("(c p) n -> p c n", p=P)).then_inc(aw_loaded, 16)
            sp.dma_start(wk_s, Wk.rearrange("(c p) n -> p c n", p=P)).then_inc(aw_loaded, 16)
            sp.dma_start(wv_s, Wv.rearrange("(c p) n -> p c n", p=P)).then_inc(aw_loaded, 16)
            sp.dma_start(bv_s, bv.partition_broadcast(P)).then_inc(aw_loaded, 16)
            sp.dma_start(qkb[:, 0, :], bq.rearrange("(c p) -> p c", p=P), allow_slow_non_contiguous=True).then_inc(aw_loaded, 16)
            sp.dma_start(qkb[:, 1, :], bk.rearrange("(c p) -> p c", p=P), allow_slow_non_contiguous=True).then_inc(aw_loaded, 16)
            for j in range(HQ):
                sp.dma_start(wo_s[HS * j:HS * j + HD, :, :],
                             Wo.rearrange("(q j i) n -> j i q n", q=NQ, j=HQ)[j]).then_inc(aw_loaded, 16)
            sp.dma_start(wo_s[HD:HD + 1, 0, :], bo.rearrange("(a n) -> a n", a=1)).then_inc(aw_loaded, 16)
            with sp.Fori(0, B) as b:
                sp.wait_ge(s_done, b * UNITS + OPEN)
                sp.wait_ge(k_ready, b * DC + DC)
                for h in range(H):
                    r = HD * (h % HC)
                    sp.dma_start(km[r:r + HD, h, :], kt[r:r + HD, h // HC, :]).then_inc(km_loaded, 16)
            sp.wait_ge(res_attn, B * TB + OPEN)
            load_gate_up()
            ffn(1)
            with sp.Fori(0, NT) as t:
                sp.wait_ge(res_ready, t + (NT + 1))
                sp.dma_start(out[bass.ds(t * P, P), :], res[:, bass.ds(t, 1), :]).then_inc(out_stored, 16)
            sp.wait_ge(out_stored, 16 * NT)

        @block.gpsimd
        def _(pool):
            pool.sem_inc(w_taken, OPEN)
            pool.memset(big[:], 0.0).then_inc(zero_made, 1)
            pool.memset(ident[:], 0.0).then_inc(const_made, 1)
            pool.memset(tri[:], 1.0).then_inc(const_made, 1)
            pool.memset(ones[:], 1.0).then_inc(const_made, 1)
            pool.iota(tile_no[:], pattern=[[1, NS]], base=0, channel_multiplier=0,
                      allow_small_or_imprecise_dtypes=True).then_inc(const_made, 1)
            pool.wait_ge(const_made, 4)
            pool.affine_select(out=ident[:], in_=ident[:], compare_op=ALU.not_equal, fill=1.0, base=0,
                               pattern=[[-1, P]], channel_multiplier=1).then_inc(const_made, 1)
            pool.affine_select(out=tri[:], in_=tri[:], compare_op=ALU.is_gt, fill=0.0, base=0,
                               pattern=[[1, P]], channel_multiplier=-1).then_inc(const_made, 1)

            def scatter(n):
                pool.wait_ge(pos_ready, n + 1)
                if n == 0:
                    pool.wait_ge(rows_zeroed, 16)
                for t in range(NT):
                    pool.indirect_dma_start(sorted_rows, bass.IndirectOffsetOnAxis(ap=pos[:, t:t + 1], axis=0),
                                            rows[:, t, :], None).then_inc(scattered, 16)

            def ffn(n):
                t0 = n * NS

                def take_weights(j):
                    pool.wait_ge(xs_loaded, (j + (t0 + 1)) * 16)
                    at_ = wts[:, j, :] if type(j) is int else wts[:, bass.ds(j, 1), :].rearrange("p a e -> p (a e)")
                    pool.tensor_copy(at_, xs[:, D:RW]).then_inc(w_taken, 1)

                def store(j):
                    pool.wait_ge(y_ready, j + (t0 + 1) + OPEN)
                    if type(j) is not int or j + t0:
                        pool.wait_ge(y_stored, (j + t0) * 16)
                    if type(j) is int:
                        pool.dma_start(sorted_out[j * P:(j + 1) * P, :], rows[:, j, 0:D]).then_inc(y_stored, 16)
                    else:
                        pool.dma_start(sorted_out[bass.ds(j * P, P), :], rows[:, bass.ds(j, 1), 0:D]).then_inc(y_stored, 16)

                take_weights(0)
                take_weights(1)
                take_weights(2)
                store(0)
                with pool.Fori(3, NS) as j:
                    take_weights(j)
                    store(j - 2)
                store(NS - 2)
                store(NS - 1)

            def gather(n):
                pool.wait_ge(y_stored, 16 * NS * (n + 1))
                for t in range(NT):
                    if t or n:
                        pool.wait_ge(y_gathered, 16 * (t + n * NT))
                    pool.indirect_dma_start(rows[:, t, 0:D], None, sorted_out,
                                            bass.IndirectOffsetOnAxis(ap=pos[:, t:t + 1], axis=0)).then_inc(y_gathered, 16)

            scatter(0)
            ffn(0)
            pool.wait_ge(y_ready, NS + OPEN)
            pool.memset(va[:], 0.0).then_inc(pads_made, 1)
            pool.memset(wo_s[:], 0.0).then_inc(pads_made, 1)
            pool.wait_ge(pads_made, 2)
            pool.memset(va[:, :, 0, HD:HD + 1], 1.0).then_inc(pads_made, 1)
            last = S // STRIDE
            for k in range(last):
                n_over = (1 if k in (0, last - 1) else 2) + (1 if k >= last - 2 else 0)
                pool.memset(inv_count[:, k * STRIDE:(k + 1) * STRIDE], 1.0 / n_over).then_inc(acon_ready, 1)
            gather(0)
            pool.wait_ge(res_ready, NT)
            pool.memset(km[:], 0.0).then_inc(pads_made, 1)
            with pool.Fori(0, B) as b:
                pool.wait_ge(o_done, b * TB + OPEN)
                pool.sem_inc(batch_open, 1)
                pool.memset(ctxt[:], 0.0).then_inc(acc_zero, 1)
                pool.wait_ge(acc_zero, b + 1)
                for n in range(NWIN):
                    pool.wait_ge(ct_ready, b * NWIN + n + 1)
                    if n:
                        pool.wait_ge(acc_done, b * NWIN + n)
                    win = ctxt[:, :, n * STRIDE:n * STRIDE + W]
                    pool.tensor_tensor(win, win, ct[:, n % 2], ALU.add).then_inc(acc_done, 1)
                pool.wait_ge(acc_done, b * NWIN + NWIN)
                pool.tensor_tensor(ctxt[:], ctxt[:], inv_count.unsqueeze(1).to_broadcast([P, NQ, S]),
                                   ALU.mult).then_inc(ctx_ready, 1)
            scatter(1)
            ffn(1)
            gather(1)

        @block.scalar
        def _(act):
            act.sem_inc(rt_ready, OPEN)
            act.sem_inc(ht0_ready, OPEN)
            def std(n):
                nc.scalar.preload_act_table(ACT.Sqrt)
                act.wait_ge(var_ready, n + 1)
                nc.scalar.activation(ln_t[:, 0, :], ln_t[:, 1, :], ACT.Sqrt).then_inc(std_ready, 1)

            def route(n):
                with act.Fori(0, NT // 2) as i:
                    for k in range(2):
                        act.wait_ge(rt_psum, i * 2 + (n * NT + k + 1) + OPEN)
                        nc.scalar.copy(rt[:, k], bank[k][:, 0:D].rearrange("p (c t) -> p c t", c=DC)).then_inc(rt_ready, 1)
                nc.scalar.preload_act_table(ACT.Sigmoid)
                act.wait_ge(logits_done, NT * (n + 1))
                nc.scalar.activation(sg[:], bank[2][:, 0:NT * NR].rearrange("p (t r) -> p t r", r=NR),
                                     ACT.Sigmoid).then_inc(sig_ready, 1)

            def ffn(n):
                t0 = n * NS

                def silu(j, e):
                    act.wait_ge(gu_done, j * E + (t0 * E + e + 1))
                    act.wait_ge(h_ready, j * E + (t0 * E + e - 1))
                    nc.scalar.activation(sl[:, e], bank[2 * e][:], ACT.Silu).then_inc(silu_done, 1)

                def silu_first(e):
                    act.wait_ge(gu_done, t0 * E + e + 1)
                    nc.scalar.activation(sl[:, e], bank[2 * e][:], ACT.Silu).then_inc(silu_done, 1)

                def xt_evac(j):
                    act.wait_ge(xt_psum, j + (t0 + 1) + OPEN)
                    nc.scalar.copy(xt[:], bank[7][:, 0:D].rearrange("p (c t) -> p c t", c=DC)).then_inc(xt_ready, 1)

                def ht_evac(j):
                    act.wait_ge(ht_psum, j * E + (t0 * E + 1))
                    nc.scalar.copy(ht[:, 0], bank[4][:]).then_inc(ht0_ready, 1)

                nc.scalar.preload_act_table(ACT.Silu)
                xt_evac(0)
                silu_first(0)
                silu_first(1)
                xt_evac(1)
                ht_evac(0)
                with act.Fori(1, NS - 1) as j:
                    silu(j, 0)
                    silu(j, 1)
                    xt_evac(j + 1)
                    ht_evac(j)
                silu(NS - 1, 0)
                silu(NS - 1, 1)
                ht_evac(NS - 1)

            std(0)
            route(0)
            ffn(0)

            std(1)
            nc.scalar.preload_act_table(ACT.Exp)
            act.wait_ge(aw_loaded, 16 * (8 + HQ))
            nc.scalar.mul(qkb[:, 2, :], qkb[:, 0, :], -1.0 / HD ** 0.5).then_inc(act_step, 1)
            act.wait_ge(act_step, 1)
            with act.Fori(0, B) as b:
                act.wait_ge(xnt_psum, b * DC + 1 + OPEN)
                nc.scalar.copy(xnt[:, 0, :], bank[6][:]).then_inc(xnt0_ready, 1)
                for m in range(DC):
                    act.wait_ge(proj_done, b * 11 + (m + 1))
                    nc.scalar.activation(qt[:, m, :], bank[6 + m][:], ACT.Identity, bias=qkb[:, 2, m:m + 1],
                                         scale=-1.0 / HD ** 0.5).then_inc(q_ready, 1)
                for u in range(UNITS):
                    act.wait_ge(sb_ready, b * UNITS + (u + 1))
                    if u >= 2:
                        act.wait_ge(pt_psum, b * UNITS + (u - 1))
                    for h in range(HQ):
                        a = nc.scalar.activation(prob[:, u % 2, h], sbuf_s[:, u % 2, h], ACT.Exp,
                                                 bias=nmax[:, u % 2, h:h + 1], scale=-1.0)
                    a.then_inc(p_ready, 1)

            std(2)
            route(1)
            ffn(1)

        @block.tensor
        def _(pe):
            pe.sem_inc(s_done, OPEN)
            pe.sem_inc(xt_psum, OPEN)
            pe.sem_inc(o_done, OPEN)
            pe.sem_inc(rt_psum, OPEN)
            pe.sem_inc(xnt_psum, OPEN)
            def transpose(dst, src):
                return nc.tensor.transpose(dst, src, ident[:])

            def route(n):
                for_lg = bank[2]
                with pe.Fori(0, NT // 2) as i:
                    for k in range(2):
                        pe.wait_ge(x2_ready, i * 2 + (n * NT + k + 1))
                        pe.wait_ge(rt_ready, i * 2 + n * NT + OPEN)
                        for c in range(DC):
                            tr = transpose(bank[k][:, c * P:(c + 1) * P],
                                           xn2[:, k, c * P:(c + 1) * P])
                        tr.then_inc(rt_psum, 1)
                    for k in range(2):
                        pe.wait_ge(rt_ready, i * 2 + (n * NT + k + 1) + OPEN)
                        for c in range(DC):
                            mm = nc.tensor.matmul(for_lg[:, bass.ds((i * 2 + k) * NR, NR)], rt[:, k, c, :], wr[:, c, :],
                                                  start=(c == 0), stop=(c == DC - 1))
                        mm.then_inc(logits_done, 1)
                pe.wait_ge(onehot_ready, n + 1)
                nc.tensor.matmul(bank[3][:, 0:G * NT], tri[:], oh[:].rearrange("p g t -> p (g t)"), start=True, stop=True)
                nc.tensor.matmul(bank[4][:, 0:G * NT], ones[:], oh[:].rearrange("p g t -> p (g t)"),
                                 start=True, stop=True).then_inc(rank_done, 1)

            def ffn(n):
                t0 = n * NS

                def tx(j):
                    pe.wait_ge(xs_loaded, (j + (t0 + 1)) * 16)
                    pe.wait_ge(xt_ready, j + t0)
                    for c in range(DC):
                        tr = transpose(bank[7][:, c * P:(c + 1) * P], xs[:, c * P:(c + 1) * P])
                    tr.then_inc(xt_psum, 1)

                def gate_up(j, g, e, first=False):
                    pe.wait_ge(xt_ready, j + (t0 + 1))
                    if not first:
                        pe.wait_ge(h_ready, j * E + (t0 * E + e - 1))
                    for bk_, w in ((bank[2 * e], wg), (bank[2 * e + 1], wu)):
                        for c in range(DC):
                            mm = nc.tensor.matmul(bk_[:], xt[:, c, :],
                                                  w[:, c, bass.ds(g * E + e, 1), :].rearrange("p a f -> p (a f)"),
                                                  start=(c == 0), stop=(c == DC - 1))
                    mm.then_inc(gu_done, 1)

                def th(j, e):
                    pe.wait_ge(h_ready, j * E + (t0 * E + e + 1))
                    pe.wait_ge((ht0_ready, ht1_ready)[e], j + t0 + OPEN)
                    for f in range(FC):
                        tr = transpose(bank[4 + e][:, f * P:(f + 1) * P], hb[:, e, f * P:(f + 1) * P])
                    tr.then_inc(ht_psum, 1)

                def down(j, g, e):
                    pe.wait_ge((ht0_ready, ht1_ready)[e], j + (t0 + 1) + OPEN)
                    if e == 0:
                        pe.wait_ge(y_ready, j + t0 + OPEN)
                    for f in range(FC):
                        mm = nc.tensor.matmul(bank[6][:, 0:D], ht[:, e, f * P:(f + 1) * P],
                                              wd[:, f, bass.ds(g * E + e, 1), :].rearrange("p a n -> p (a n)"),
                                              start=(e == 0 and f == 0), stop=(e == E - 1 and f == FC - 1))
                    if e == E - 1:
                        mm.then_inc(d_done, 1)

                def group(j):
                    at_ = tile_group[0:1, j:j + 1] if type(j) is int else tile_group[0:1, bass.ds(j, 1)]
                    return pe.value_load(at_, min_val=0, max_val=G - 1)

                pe.wait_ge(pos_ready, n + 1)
                pe.wait_ge(w_loaded, 16 * (3 if n == 0 else 5) * NEXP)
                tx(0)
                g0 = group(0)
                gate_up(0, g0, 0, first=True)
                gate_up(0, g0, 1, first=True)
                tx(1)
                th(0, 0)
                with pe.Fori(1, NS - 1) as j:
                    ga = group(j)
                    gb = group(j - 1)
                    gate_up(j, ga, 0)
                    th(j - 1, 1)
                    down(j - 1, gb, 0)
                    gate_up(j, ga, 1)
                    tx(j + 1)
                    th(j, 0)
                    down(j - 1, gb, 1)
                j = NS - 1
                ga, gb = group(j), group(j - 1)
                gate_up(j, ga, 0)
                th(j - 1, 1)
                down(j - 1, gb, 0)
                gate_up(j, ga, 1)
                th(j, 0)
                down(j - 1, gb, 1)
                th(j, 1)
                down(j, ga, 0)
                down(j, ga, 1)

            pe.wait_ge(const_made, 6)
            pe.wait_ge(wr_loaded, 16 * (1 + G))
            route(0)
            ffn(0)

            pe.wait_ge(aw_loaded, 16 * (8 + HQ))
            pe.wait_ge(pads_made, 4)
            with pe.Fori(0, B) as b:
                for c in range(DC):
                    pe.wait_ge(xa_ready, b * TB + TB)
                    if c == 0:
                        pe.wait_ge(res_attn, b * TB + OPEN)
                    for t in range(TB):
                        tr = transpose(bank[6 + c][:, t * P:(t + 1) * P], xa[:, t, c * P:(c + 1) * P])
                    tr.then_inc(xnt_psum, 1)
                pe.wait_ge(xnt0_ready, b + 1)
                pe.wait_ge(xnt1_ready, b + 1)
                for i, (w, m) in enumerate([(wq_s, 0), (wq_s, 1), (wk_s, 0), (wk_s, 1)]):
                    if i >= 2:
                        pe.wait_ge(q_ready, b * DC + (i - 1))
                    for c in range(DC):
                        mm = nc.tensor.matmul(bank[6 + m][:], w[:, c, m * P:(m + 1) * P], xnt[:, c, :],
                                              start=(c == 0), stop=(c == DC - 1))
                    mm.then_inc(proj_done, 1)
                for n in range(NWIN):
                    if n < 2:
                        pe.wait_ge(k_ready, b * DC + (n + 1))
                    else:
                        pe.wait_ge(v_ready, b * NWIN + (n - 1))
                    for c in range(DC):
                        mm = nc.tensor.matmul(bank[6 + n % 2][:, 0:D], xnt[:, c, n * STRIDE:n * STRIDE + W], wv_s[:, c, :],
                                              start=(c == 0), stop=(c == DC - 1))
                    mm.then_inc(proj_done, 1)

                def scores(u):
                    n, q = divmod(u, NQ)
                    if u == 0:
                        pe.wait_ge(km_loaded, (b + 1) * (16 * H) + OPEN)
                        pe.wait_ge(q_ready, (b + 1) * DC)
                    if u >= 2:
                        pe.wait_ge(sb_ready, b * UNITS + (u - 1))
                    nc.tensor.matmul(bank[u % 2][:].rearrange("p (h k) -> p h k", h=HQ),
                                     qt[:, q * HQ // HC, n * STRIDE:n * STRIDE + W],
                                     km[:, q * HQ:(q + 1) * HQ, n * STRIDE:n * STRIDE + W],
                                     start=True, stop=True).then_inc(s_done, 1)

                def turn(u):
                    pe.wait_ge(p_ready, b * UNITS + (u + 1))
                    if u >= 2:
                        pe.wait_ge(pt_ready, b * UNITS + (u - 1))
                    for h in range(HQ):
                        tr = transpose(bank[2 + u % 2][:, h * W:(h + 1) * W], prob[:, u % 2, h])
                    tr.then_inc(pt_psum, 1)

                def values(u):
                    n, q = divmod(u, NQ)
                    if u == 0:
                        pe.wait_ge(v_ready, (b + 1) * NWIN)
                    if n and q == 0:
                        pe.wait_ge(ct_ready, b * NWIN + n)
                    pe.wait_ge(pt_ready, b * UNITS + (u + 1))
                    for h in range(HQ):
                        nc.tensor.matmul(bank[4][HS * h:HS * (h + 1), q * W:(q + 1) * W], va[:, n, q * HQ + h, :],
                                         pt_s[:, u % 2, h * W:(h + 1) * W], start=True, stop=True)
                        mm = nc.tensor.matmul(bank[5][HS * h:HS * (h + 1), q * W:(q + 1) * W], ones[:, 0:HS],
                                              pt_s[:, u % 2, h * W:(h + 1) * W], start=True, stop=True)
                    mm.then_inc(pv_done, 1)

                scores(0)
                scores(1)
                for u in range(UNITS):
                    turn(u)
                    if u + 2 < UNITS:
                        scores(u + 2)
                    if u:
                        values(u - 1)
                values(UNITS - 1)
                pe.wait_ge(ctx_ready, b + 1)
                for t in range(TB):
                    if t >= 2:
                        pe.wait_ge(res_attn, b * TB + (t - 1) + OPEN)
                    for q in range(NQ):
                        mm = nc.tensor.matmul(bank[6 + t % 2][:, 0:D], ctxt[:, q, t * P:(t + 1) * P], wo_s[:, q, :],
                                              start=(q == 0), stop=(q == NQ - 1))
                    mm.then_inc(o_done, 1)

            route(1)
            ffn(1)

        @block.vector
        def _(dve):
            dve.sem_inc(ht1_ready, OPEN)
            dve.sem_inc(y_ready, OPEN)
            dve.sem_inc(res_attn, OPEN)
            steps = [0]

            def then(ins):
                steps[0] += 1
                ins.then_inc(dve_step, 1)
                dve.wait_ge(dve_step, steps[0])

            def bc(v, n):
                return v.unsqueeze(1).to_broadcast([P, n, v.shape[-1]])

            def layer_stats(n):
                with dve.Fori(0, NT) as t:
                    if n == 0:
                        pass
                    nc.vector.bn_stats(stats[:, bass.ds(t, 1), :].rearrange("p a s -> p (a s)"),
                                       res[:, bass.ds(t, 1), :].rearrange("p a d -> p (a d)")).then_inc(stats_done, 1)
                dve.wait_ge(stats_done, NT * (n + 1))
                a, v, d, dd = (ln_t[:, i, :] for i in range(4))
                then(nc.vector.tensor_tensor(a, stats[:, :, 1], stats[:, :, 4], ALU.add))
                then(nc.vector.tensor_scalar(mean[:], a, 0.5, None, ALU.mult))
                then(nc.vector.tensor_tensor(d, stats[:, :, 1], stats[:, :, 4], ALU.subtract))
                then(nc.vector.tensor_scalar(d, d, 0.5, None, ALU.mult))
                then(nc.vector.tensor_tensor(dd, d, d, ALU.mult))
                then(nc.vector.tensor_tensor(a, stats[:, :, 2], stats[:, :, 5], ALU.add))
                then(nc.vector.tensor_scalar(a, a, 1.0 / D, LN_EPS, ALU.mult, ALU.add))
                nc.vector.tensor_tensor(v, a, dd, ALU.add).then_inc(var_ready, 1)
                dve.wait_ge(std_ready, n + 1)
                then(nc.vector.reciprocal(rstd[:], a))

            def route(n):
                with dve.Fori(0, NT // 2) as i:
                    for k in range(2):
                        dve.wait_ge(rt_psum, i * 2 + n * NT + OPEN)
                        t = i * 2 + k
                        for dst, done in ((xn2[:, k], x2_ready), (rows[:, bass.ds(t, 1), 0:D].rearrange("p a d -> p (a d)"), xn_ready)):
                            nc.vector.tensor_scalar(dst, res[:, bass.ds(t, 1), :].rearrange("p a d -> p (a d)"),
                                                    mean[:, bass.ds(t, 1)], rstd[:, bass.ds(t, 1)],
                                                    ALU.subtract, ALU.mult).then_inc(done, 1)
                dve.wait_ge(sig_ready, n + 1)
                best, left, den, u0, u1, t0, t1, mv = (rsc[:, i, :] for i in range(8))
                then(nc.vector.tensor_reduce(best, sg[:, :, 0:G], AX.X, ALU.max))
                then(nc.vector.tensor_tensor(oh[:, 0], sg[:, :, 0], best, ALU.is_ge))
                then(nc.vector.tensor_scalar(left, oh[:, 0], -1.0, 1.0, ALU.mult, ALU.add))
                for g in range(1, G - 1):
                    then(nc.vector.tensor_tensor(t0, sg[:, :, g], best, ALU.is_ge))
                    then(nc.vector.tensor_tensor(oh[:, g], t0, left, ALU.mult))
                    then(nc.vector.tensor_tensor(left, left, oh[:, g], ALU.subtract))
                nc.vector.tensor_copy(oh[:, G - 1], left).then_inc(onehot_ready, 1)
                dve.wait_ge(onehot_ready, n + 1)
                for e, u in ((0, u0), (1, u1)):
                    then(nc.vector.tensor_tensor(u, oh[:, 0], sg[:, :, G + e], ALU.mult))
                    for g in range(1, G):
                        then(nc.vector.tensor_tensor(t0, oh[:, g], sg[:, :, G + E * g + e], ALU.mult))
                        then(nc.vector.tensor_tensor(u, u, t0, ALU.add))
                then(nc.vector.tensor_scalar(t0, best, TOPK_EPS, None, ALU.add))
                then(nc.vector.reciprocal(t1, t0))
                then(nc.vector.tensor_tensor(mv, best, t1, ALU.mult))
                then(nc.vector.tensor_tensor(t0, u0, u1, ALU.add))
                then(nc.vector.tensor_scalar(t0, t0, TOPK_EPS, None, ALU.add))
                then(nc.vector.reciprocal(t1, t0))
                then(nc.vector.tensor_tensor(mv, mv, t1, ALU.mult))
                then(nc.vector.tensor_tensor(rows[:, 0:NT, D], mv, u0, ALU.mult))
                then(nc.vector.tensor_tensor(rows[:, 0:NT, D + 1], mv, u1, ALU.mult))
                dve.wait_ge(rank_done, n + 1)
                then(nc.vector.tensor_copy(cnt[:], bank[4][:, 0:G * NT].rearrange("p (g t) -> p g t", g=G)))
                for g in range(G):
                    then(nc.vector.tensor_tensor_scan(pre[:, g], ones[:, 0:NT], cnt[:, g], 0.0, ALU.mult, ALU.add))
                need, base = gsc[:, 0], gsc[:, 1]
                then(nc.vector.tensor_scalar(gint[:, 0], pre[:, :, NT - 1], float(P - 1), None, ALU.add))
                then(nc.vector.tensor_single_scalar(gint[:, 1], gint[:, 0], 7, ALU.arith_shift_right))
                then(nc.vector.tensor_copy(need, gint[:, 1]))
                then(nc.vector.memset(base, 0.0))
                for g in range(1, G):
                    then(nc.vector.tensor_tensor(base[:, g:g + 1], base[:, g - 1:g], need[:, g - 1:g], ALU.add))
                then(nc.vector.tensor_scalar(gsc[:, 2], base, float(P), None, ALU.mult))
                then(nc.vector.tensor_tensor(pre[:], pre[:], cnt[:], ALU.subtract))
                then(nc.vector.tensor_tensor(pre[:], pre[:], bank[3][:, 0:G * NT].rearrange("p (g t) -> p g t", g=G), ALU.add))
                then(nc.vector.tensor_tensor(pre[:], pre[:], gsc[:, 2].unsqueeze(2).to_broadcast([P, G, NT]), ALU.add))
                then(nc.vector.tensor_tensor(pre[:], pre[:], oh[:], ALU.mult))
                then(nc.vector.tensor_reduce(posf[:], pre[:].rearrange("p g t -> p t g"), AX.X, ALU.add))
                then(nc.vector.tensor_copy(pos[:], posf[:]))
                a, b_ = tgrp_f[:, 0], tgrp_f[:, 1]
                then(nc.vector.tensor_scalar(a, tile_no[:], base[:, 1:2], None, ALU.is_ge))
                for g in range(2, G):
                    then(nc.vector.tensor_scalar(b_, tile_no[:], base[:, g:g + 1], None, ALU.is_ge))
                    then(nc.vector.tensor_tensor(a, a, b_, ALU.add))
                nc.vector.tensor_copy(tile_group[:], a).then_inc(pos_ready, 1)

            def ffn(n):
                t0 = n * NS

                def at_tile(j, lo, hi):
                    if type(j) is int:
                        return rows[:, j, lo:hi]
                    return rows[:, bass.ds(j, 1), lo:hi].rearrange("p a d -> p (a d)")

                def weight(j, e):
                    if type(j) is int:
                        return wts[:, j, e:e + 1]
                    return wts[:, bass.ds(j, 1), e:e + 1].rearrange("p a d -> p (a d)")

                def product(j, e, first=False):
                    dve.wait_ge(silu_done, j * E + (t0 * E + e + 1))
                    if not first:
                        dve.wait_ge(ht_psum, j * E + (t0 * E + e - 1))
                    nc.vector.scalar_tensor_tensor(out=hb[:, e], in0=bank[2 * e + 1][:], scalar=weight(j, e),
                                                   in1=sl[:, e], op0=ALU.mult, op1=ALU.mult).then_inc(h_ready, 1)

                def ht_evac(j):
                    dve.wait_ge(ht_psum, j * E + (t0 * E + 2))
                    nc.vector.tensor_copy(ht[:, 1], bank[5][:]).then_inc(ht1_ready, 1)

                def y_evac(j):
                    dve.wait_ge(d_done, j + (t0 + 1))
                    nc.vector.tensor_copy(at_tile(j, 0, D), bank[6][:, 0:D]).then_inc(y_ready, 1)

                dve.wait_ge(w_taken, t0 + 1 + OPEN)
                product(0, 0, first=True)
                product(0, 1, first=True)
                with dve.Fori(1, NS - 1) as j:
                    ht_evac(j - 1)
                    dve.wait_ge(w_taken, j + (t0 + 1) + OPEN)
                    product(j, 0)
                    product(j, 1)
                    y_evac(j - 1)
                j = NS - 1
                ht_evac(j - 1)
                dve.wait_ge(w_taken, j + (t0 + 1) + OPEN)
                product(j, 0)
                product(j, 1)
                y_evac(j - 1)
                ht_evac(j)
                y_evac(j)
                with dve.Fori(0, NT) as t:
                    dve.wait_ge(y_gathered, (t + (n * NT + 1)) * 16)
                    nc.vector.scalar_tensor_tensor(out=res[:, bass.ds(t, 1), :], in0=rows[:, bass.ds(t, 1), 0:D], scalar=0.5,
                                                   in1=res[:, bass.ds(t, 1), :], op0=ALU.mult, op1=ALU.add).then_inc(res_ready, 1)

            dve.wait_ge(x_loaded, 16 * B)
            dve.wait_ge(const_made, 6)
            dve.wait_ge(zero_made, 1)
            dve.wait_ge(rows_zeroed, 16)
            layer_stats(0)
            route(0)
            ffn(0)

            dve.wait_ge(res_ready, NT)
            layer_stats(1)
            dve.wait_ge(aw_loaded, 16 * (8 + HQ))
            then(nc.vector.tensor_scalar(nbias[:], nbias[:], -1.0, None, ALU.mult))
            with dve.Fori(0, B) as b:
                if True:
                    dve.wait_ge(xnt_psum, b * DC + OPEN)
                for t in range(TB):
                    nc.vector.tensor_scalar(xa[:, t, :], res[:, bass.ds(b * TB + t, 1), :].rearrange("p a d -> p (a d)"),
                                            mean[:, bass.ds(b * TB + t, 1)], rstd[:, bass.ds(b * TB + t, 1)],
                                            ALU.subtract, ALU.mult).then_inc(xa_ready, 1)
                dve.wait_ge(xnt_psum, b * DC + DC + OPEN)
                nc.vector.tensor_copy(xnt[:, 1, :], bank[7][:]).then_inc(xnt1_ready, 1)
                dve.wait_ge(km_loaded, b * (16 * H) + OPEN)
                for m in range(DC):
                    dve.wait_ge(proj_done, b * 11 + (DC + m + 1))
                    nc.vector.tensor_scalar(kt[:, m, :], bank[6 + m][:], qkb[:, 1, m:m + 1], None, ALU.add).then_inc(k_ready, 1)
                for n in range(NWIN):
                    dve.wait_ge(proj_done, b * 11 + (2 * DC + n + 1))
                    nc.vector.tensor_tensor(va[:, n, :, 0:HD], bank[6 + n % 2][:, 0:D].rearrange("p (h i) -> p h i", h=H),
                                            bv_s.rearrange("p (h i) -> p h i", h=H), ALU.add).then_inc(v_ready, 1)

                def biased(u):
                    dve.wait_ge(s_done, b * UNITS + (u + 1) + OPEN)
                    if u >= 2:
                        dve.wait_ge(p_ready, b * UNITS + (u - 1))
                    dve.sem_inc(unit_open, 1)
                    for h in range(HQ):
                        i = nc.vector.tensor_tensor_reduce(out=sbuf_s[:, u % 2, h], in0=bank[u % 2][:, h * W:(h + 1) * W],
                                                           in1=nbias[:, (u % NQ) * HQ + h], scale=1.0, scalar=BIG,
                                                           op0=ALU.add, op1=ALU.min, accum_out=nmax[:, u % 2, h:h + 1])
                    i.then_inc(sb_ready, 1)

                def pt_evac(u):
                    dve.wait_ge(pt_psum, b * UNITS + (u + 1))
                    if u >= 2:
                        dve.wait_ge(pv_done, b * UNITS + (u - 1))
                    nc.vector.tensor_copy(pt_s[:, u % 2], bank[2 + u % 2][:]).then_inc(pt_ready, 1)

                def normalise(n):
                    dve.wait_ge(pv_done, b * UNITS + (n + 1) * NQ)
                    nc.vector.reciprocal(rcp[:], bank[5][:].rearrange("p (q k) -> p q k", q=NQ)).then_inc(rcp_ready, 1)
                    dve.wait_ge(rcp_ready, b * NWIN + (n + 1))
                    if n >= 2:
                        dve.wait_ge(acc_done, b * NWIN + (n - 1))
                    nc.vector.scalar_tensor_tensor(out=ct[:, n % 2], in0=bank[4][:].rearrange("p (q k) -> p q k", q=NQ),
                                                   scalar=2.0 if n == NWIN - 1 else 1.0, in1=rcp[:],
                                                   op0=ALU.mult, op1=ALU.mult).then_inc(ct_ready, 1)

                biased(0)
                biased(1)
                for u in range(UNITS):
                    pt_evac(u)
                    if u + 2 < UNITS:
                        biased(u + 2)
                    if u % NQ == 1 and u > NQ:
                        normalise(u // NQ - 1)
                normalise(NWIN - 1)
                for t in range(TB):
                    dve.wait_ge(o_done, b * TB + (t + 1) + OPEN)
                    tile = res[:, bass.ds(b * TB + t, 1), :].rearrange("p a d -> p (a d)")
                    i = nc.vector.tensor_tensor(tile, bank[6 + t % 2][:, 0:D], tile, ALU.add)
                    i.then_inc(res_attn, 1)

            dve.wait_ge(res_attn, B * TB + OPEN)
            layer_stats(2)
            route(1)
            ffn(1)


_INS = ['L0_attn_hidden_states', 'L0_attn_Wq', 'L0_attn_bq', 'L0_attn_Wk', 'L0_attn_bk', 'L0_attn_Wv', 'L0_attn_bv',
        'L0_attn_Wo', 'L0_attn_bo', 'L0_attn_pos_bias', 'L0_ffn_macro_w', 'L0_ffn_micro_w', 'L0_ffn_gate_w',
        'L0_ffn_up_w', 'L0_ffn_down_w']


def kernel(**inputs):
    import numpy as _np
    import concourse.bacc as _bacc
    from concourse import mybir as _mybir
    from concourse.bass_utils import run_bass_kernel_spmd as _run

    nc = _bacc.Bacc("TRN2", target_bir_lowering=False, num_devices=1)
    arrays, args = {}, []
    for name in _INS:
        a = _np.ascontiguousarray(inputs[name])
        arrays[f"in_{name}"] = a
        args.append(nc.dram_tensor(f"in_{name}", a.shape, _mybir.dt.from_np(a.dtype), kind="ExternalInput").ap())
    args.append(nc.dram_tensor("out_0", (T, D), F32, kind="ExternalOutput").ap())
    macaron_kernel(nc, *args)
    r = _run(nc, [arrays], core_ids=[0])
    return r.results[0]["out_0"].reshape(B, S, D)
```

```python
import concourse.bass as bass
from concourse import mybir
from contextlib import ExitStack

F32 = mybir.dt.float32
I32 = mybir.dt.int32
ALU = mybir.AluOpType
ACT = mybir.ActivationFunctionType
AX = mybir.AxisListType

P = 128
B, S, D = 8, 512, 256
T = B * S
NT = T // P
TB = S // P
DC = D // P
F = 512
FC = F // P
G, E = 4, 2
NEXP = G * E
NS = NT + G - 1
NR = G + NEXP
C_W, C_MEAN, C_RSTD, C_TOK, RW = D, D + 2, D + 3, D + 4, D + 5
CAP = T + P
SPARE = G * CAP
H, HD = 16, 16
W, STRIDE = 128, 64
NWIN = (S - W) // STRIDE + 1
HQ = 4
NQ = H // HQ
UNITS = NWIN * NQ
HS = 2 * HD
NB = 4
HC = P // HD
LN_EPS = 1e-5
TOPK_EPS = 1e-9
BIG = 3.0e38
OPEN = 1
NORM_STEPS, ROUTE_STEPS, TABLE_STEPS = 3, 21, 18
CONSTS = 6 + 2 * G + 3 + 3
NPROJ = 2 * DC + TB
ATTN_LOADS = 9
SHIFTS = NWIN - 1


def macaron_kernel(nc, x_in, Wq, bq, Wk, bk, Wv, bv, Wo, bo, pos_bias, macro_w, micro_w, gate_w, up_w, down_w, out):
    ctx = ExitStack()
    with ctx:
        def sb(name, shape, dt=F32):
            return ctx.enter_context(nc.sbuf_tensor(name, shape, dt))

        def sem(name):
            return ctx.enter_context(nc.semaphore(name))

        sorted_rows = nc.dram_tensor("sorted_rows", [SPARE + P, RW], F32, kind="Internal").ap()
        mid = nc.dram_tensor("mid", [T + (G + 1) * P, D], F32, kind="Internal").ap()

        wgu = sb("wgu", [P, 2 * DC * NEXP * F])
        wd = sb("wd", [P, FC, NEXP, D])
        wg = wgu[:, 0:DC * NEXP * F].rearrange("p (c e f) -> p c e f", c=DC, e=NEXP)
        wu = wgu[:, DC * NEXP * F:].rearrange("p (c e f) -> p c e f", c=DC, e=NEXP)
        big = sb("big", [P, NS * RW])
        tiles = big[:, :].rearrange("p (t r) -> p t r", r=RW)
        tiles_i = big[:, :].bitcast(I32).rearrange("p (t r) -> p t r", r=RW)
        km = big[:, 0:H * S].rearrange("p (h s) -> p h s", h=H)

        ident = sb("ident", [P, P])
        tri = sb("tri", [P, P])
        ones = sb("ones", [P, P])
        mhalf = sb("mhalf", [P, TB])
        gweight = sb("gweight", [P, G])
        gcap = sb("gcap", [P, G])
        part_no = sb("part_no", [P, 1])
        tile_no = sb("tile_no", [P, NS])
        token_no = sb("token_no", [P, NT], I32)
        pads = sb("pads", [P, G + 1, RW])
        pads_i = pads[:].bitcast(I32)
        wr = sb("wr", [P, DC, NR])

        stage = sb("stage", [P, 2, TB, RW])
        stage_i = stage[:].bitcast(I32)
        stats = sb("stats", [P, TB, 6])
        ln_t = sb("ln_t", [P, 6, TB])
        mean_b = sb("mean_b", [P, TB])
        xa = sb("xa", [P, TB, D])
        xnt = sb("xnt", [P, DC, S])
        ex = sb("ex", [P, TB, NR])
        sg = sb("sg", [P, TB, NR])
        best = sb("best", [P, TB])
        eq = sb("eq", [P, TB, G])
        eqw = sb("eqw", [P, TB, G])
        first = sb("first", [P, TB])
        oh = sb("oh", [P, TB, G])
        seen = sb("seen", [P, TB + 1, G])
        picked = sb("picked", [P, TB, G, E])
        u01 = sb("u01", [P, TB, E])
        rs4 = sb("rs4", [P, 4, TB])
        place = sb("place", [P, TB, G])
        posf = sb("posf", [P, TB])
        pos = sb("pos", [P, 2, TB], I32)
        tot_i = sb("tot_i", [P, 2, G], I32)
        need = sb("need", [P, G])
        base = sb("base", [P, G + 1])
        jump = sb("jump", [P, G])
        padf = sb("padf", [P, G])
        pad_pos = sb("pad_pos", [P, G], I32)
        tt = sb("tt", [P, 4, NS])
        tile_group = sb("tile_group", [P, NS], I32)
        tile_start = sb("tile_start", [P, NS], I32)
        xn = sb("xn", [P, D])
        xt = sb("xt", [P, DC, P])
        sl = sb("sl", [P, E, F])
        hb = sb("hb", [P, E, F])
        ht = sb("ht", [P, E, F])
        yt = sb("yt", [P, D])
        yidx = sb("yidx", [P, 1], I32)

        at = [0]

        def part(*shape):
            n = 1
            for k in shape:
                n *= k
            v = wgu[:, at[0]:at[0] + n]
            at[0] += n
            names = "abcd"[:len(shape)]
            if len(shape) > 1:
                v = v.rearrange(f"p ({' '.join(names)}) -> p {' '.join(names)}",
                                **{c: k for c, k in zip(names, shape)})
            return v

        nbias = part(H, W)
        wq_s, wk_s, wv_s = part(DC, D), part(DC, D), part(DC, D)
        wo_s = part(DC, D)
        bv_s = part(D)
        bo_s = part(D)
        xb = part(TB, D)
        qt = part(DC, S)
        kt = part(DC, S)
        va = part(NWIN, H, HS)
        sbias = part(NB, HQ, W)
        prob = sb("prob", [P, NB, HQ, W])
        pt_s = part(2, HQ * W)
        nmax = part(NB, HQ)
        rsum = part(2, H)
        rinv = part(H)
        rexp = part(H, HD)
        vsum = part(DC * W)
        qkb = part(3, DC)
        inv_count = part(NWIN)
        ct = sb("ct", [P, 2, DC, W])
        ctxt = sb("ctxt", [P, DC, S])

        bank = [ctx.enter_context(nc.psum_tensor(f"bank{i}", [P, 512], F32)) for i in range(8)]

        const_made, spare_written = sem("const_made"), sem("spare_written")
        x_loaded = [sem("x_loaded0"), sem("x_loaded1")]
        wr_loaded, w_loaded, w_reloaded = sem("wr_loaded"), sem("w_loaded"), sem("w_reloaded")
        norm_step, var_ready, rstd_ready = sem("norm_step"), sem("var_ready"), sem("rstd_ready")
        xa_ready, xnt_psum, xnt0_ready, xnt1_ready = sem("xa_ready"), sem("xnt_psum"), sem("xnt0_ready"), sem("xnt1_ready")
        logits_done, ex_ready, route_step = sem("logits_done"), sem("ex_ready"), sem("route_step")
        oh_ready, rank_done, pos_ready = sem("oh_ready"), sem("rank_done"), sem("pos_ready")
        scattered = [sem("scattered0"), sem("scattered1")]
        totals_done, table_step, tables_ready, pads_scattered = (sem("totals_done"), sem("table_step"),
                                                                 sem("tables_ready"), sem("pads_scattered"))
        xs_loaded, xn_ready, xt_psum, xt_ready = sem("xs_loaded"), sem("xn_ready"), sem("xt_psum"), sem("xt_ready")
        gu_done, silu_done, h_ready = sem("gu_done"), sem("silu_done"), sem("h_ready")
        ht_psum, ht0_ready, ht1_ready = sem("ht_psum"), sem("ht0_ready"), sem("ht1_ready")
        d_done, y_ready, y_scattered, y_free = sem("d_done"), sem("y_ready"), sem("y_scattered"), sem("y_free")
        aw_loaded, apads_made, nbias_ready, qb_ready, icount_made = (
            sem("aw_loaded"), sem("apads_made"), sem("nbias_ready"), sem("qb_ready"), sem("icount_made"))
        xb_loaded, res_loaded = sem("xb_loaded"), sem("res_loaded")
        proj_done, k_ready, q_ready, v_ready = sem("proj_done"), sem("k_ready"), sem("q_ready"), sem("v_ready")
        km_loaded, s_done, sb_ready, p_ready = sem("km_loaded"), sem("s_done"), sem("sb_ready"), sem("p_ready")
        pt_psum, pt_ready, pv_done = sem("pt_psum"), sem("pt_ready"), sem("pv_done")
        rinv_ready, rexp_ready, rb_done, vsum_ready, ct_ready = (
            sem("rinv_ready"), sem("rexp_ready"), sem("rb_done"), sem("vsum_ready"), sem("ct_ready"))
        va_shifted, res_biased = sem("va_shifted"), sem("res_biased")
        ctx_zero, acc_done, o_done, res_ready = sem("ctx_zero"), sem("acc_done"), sem("o_done"), sem("res_ready")
        batch_open, unit_open, scatter_open = sem("batch_open"), sem("unit_open"), sem("scatter_open")

        def prep_use(b):
            return b * 2 + (B - 1) if type(b) is not int else (B if b == 0 else B + 2 * b - 1)

        def route_use(b):
            return b * 2 + (B + 2) if type(b) is not int or b < B - 1 else 3 * B - 1


        def flat(v):
            return v.rearrange("p a d -> p (a d)")

        def steps(u):
            return SIDE.get(u, ())

        SIDE = {0: ("stats_route",), 1: ("norm_route",), 3: ("turn_route",), 4: ("copy_route",), 6: ("logits",),
                7: ("stats_prep",), 8: ("choose",), 9: ("norm_prep",), 10: ("rank",), 12: ("place",), 15: ("turn_prep",), 16: ("copy_prep",), 18: ("k0",), 19: ("k0_copy",),
                20: ("k1",), 21: ("k1_copy",)}

        block = ctx.enter_context(nc.Block())

        @block.sync
        def _(sp):
            sp.sem_inc(km_loaded, OPEN)

            def load_x(r, par):
                sp.dma_start(stage[:, par, :, 0:D], x_in[bass.ds(r, 1)].rearrange("a (t p) d -> p (a t) d", p=P)
                             if type(r) is not int else x_in[r].rearrange("(t p) d -> p t d", p=P)).then_inc(x_loaded[par], 16)

            load_x(0, 0)
            load_x(1, 1)
            sp.dma_start(wr[:, :, 0:G], macro_w.rearrange("(c p) g -> p c g", p=P)).then_inc(wr_loaded, 16)
            for g in range(G):
                sp.dma_start(wr[:, :, G + E * g:G + E * g + E],
                             micro_w[g].rearrange("(c p) e -> p c e", p=P)).then_inc(wr_loaded, 16)
            sp.wait_ge(const_made, CONSTS)
            sp.dma_start(sorted_rows[SPARE:SPARE + P, :], pads[:, G, :]).then_inc(spare_written, 16)
            with sp.Fori(1, B // 2) as i:
                for par in range(2):
                    sp.wait_ge(scattered[par], i * (16 * TB))
                    load_x(i * 2 + par, par)

            def ffn(n):
                t0 = n * NS
                sp.wait_ge(tables_ready, n + 1)
                sp.wait_ge(spare_written, 16)
                sp.wait_ge(scattered[0], 16 * TB * (B // 2 + n * B))
                sp.wait_ge(scattered[1], 16 * TB * (B // 2))
                sp.wait_ge(pads_scattered, 16 * G * (n + 1))

                def load(j):
                    at_ = tile_start[0:1, bass.ds(j, 1)] if type(j) is not int else tile_start[0:1, j:j + 1]
                    row = sp.value_load(at_, min_val=0, max_val=SPARE)
                    dst = tiles[:, j, :] if type(j) is int else flat(tiles[:, bass.ds(j, 1), :])
                    sp.dma_start(dst, sorted_rows[bass.ds(row, P), :]).then_inc(xs_loaded, 16)

                load(0)
                with sp.Fori(1, NS) as j:
                    sp.wait_ge(xs_loaded, (j + t0) * 16)
                    load(j)

            ffn(0)
            sp.wait_ge(apads_made, 2)
            sp.dma_start(wq_s, Wq.rearrange("(c p) n -> p c n", p=P)).then_inc(aw_loaded, 16)
            sp.dma_start(wk_s, Wk.rearrange("(c p) n -> p c n", p=P)).then_inc(aw_loaded, 16)
            sp.dma_start(wv_s, Wv.rearrange("(c p) n -> p c n", p=P)).then_inc(aw_loaded, 16)
            sp.dma_start(nbias, pos_bias.rearrange("h q k -> q h k")).then_inc(aw_loaded, 16)
            sp.dma_start(bv_s, bv.partition_broadcast(P)).then_inc(aw_loaded, 16)
            sp.dma_start(qkb[:, 0, :], bq.rearrange("(c p) -> p c", p=P), allow_slow_non_contiguous=True).then_inc(aw_loaded, 16)
            sp.dma_start(qkb[:, 1, :], bk.rearrange("(c p) -> p c", p=P), allow_slow_non_contiguous=True).then_inc(aw_loaded, 16)
            sp.dma_start(wo_s, Wo.rearrange("(c p) n -> p c n", p=P)).then_inc(aw_loaded, 16)
            sp.dma_start(bo_s, bo.partition_broadcast(P)).then_inc(aw_loaded, 16)

            def rows_of(b):
                if type(b) is int:
                    return mid[b * S:(b + 1) * S, :].rearrange("(t p) d -> p t d", p=P)
                return mid[bass.ds(b * S, S), :].rearrange("(t p) d -> p t d", p=P)

            def load_batch(b):
                sp.dma_start(xb, rows_of(b)).then_inc(xb_loaded, 16)

            def mask_keys(b):
                sp.wait_ge(k_ready, b * DC + DC)
                for h in range(H):
                    r = HD * (h % HC)
                    sp.dma_start(km[r:r + HD, h, :], kt[r:r + HD, h // HC, :]).then_inc(km_loaded, 16)

            def shift_values(b):
                sp.wait_ge(v_ready, b * TB + TB)
                for n in range(1, NWIN, 2):
                    sp.dma_start(va[0:STRIDE, n], va[STRIDE:W, n - 1]).then_inc(va_shifted, 16)
                    sp.dma_start(va[STRIDE:W, n], va[0:STRIDE, n + 1]).then_inc(va_shifted, 16)

            def batch(b, last):
                if not last:
                    sp.wait_ge(xa_ready, (prep_use(b) + 1) * TB)
                    load_batch(b + 1)
                sp.wait_ge(scattered[0], b * (16 * TB) + 16 * TB * (B // 2))
                sp.dma_start(stage[:, 0, :, 0:D], rows_of(b)).then_inc(res_loaded, 16)
                if not last:
                    sp.wait_ge(s_done, b * UNITS + UNITS + OPEN)
                    mask_keys(b + 1)
                    shift_values(b + 1)

            sp.wait_ge(y_scattered, 16 * NS)
            load_batch(0)
            mask_keys(0)
            shift_values(0)
            batch(0, False)
            with sp.Fori(1, B - 1) as b:
                batch(b, False)
            batch(B - 1, True)
            sp.wait_ge(res_ready, B * TB + OPEN)
            for e in range(NEXP):
                sp.dma_start(wg[:, :, e, :], gate_w[e].rearrange("(c p) f -> p c f", p=P)).then_inc(w_reloaded, 16)
                sp.dma_start(wu[:, :, e, :], up_w[e].rearrange("(c p) f -> p c f", p=P)).then_inc(w_reloaded, 16)
            ffn(1)
            sp.wait_ge(y_scattered, 16 * NS * 2)

        @block.gpsimd
        def _(pool):
            for v, c in ((ident, 0.0), (tri, 1.0), (ones, 1.0), (mhalf, -0.5), (pads, 0.0), (seen, 0.0)):
                pool.memset(v[:], c).then_inc(const_made, 1)
            for g in range(G):
                pool.memset(gweight[:, g:g + 1], float(G - g)).then_inc(const_made, 1)
                pool.memset(gcap[:, g:g + 1], float(g * CAP)).then_inc(const_made, 1)
            pool.iota(tile_no[:], pattern=[[1, NS]], base=0, channel_multiplier=0,
                      allow_small_or_imprecise_dtypes=True).then_inc(const_made, 1)
            pool.iota(part_no[:], pattern=[[1, 1]], base=0, channel_multiplier=1,
                      allow_small_or_imprecise_dtypes=True).then_inc(const_made, 1)
            pool.iota(token_no[:], pattern=[[P, NT]], base=0, channel_multiplier=1).then_inc(const_made, 1)
            pool.wait_ge(const_made, 6 + 2 * G + 3)
            pool.affine_select(out=ident[:], in_=ident[:], compare_op=ALU.not_equal, fill=1.0, base=0,
                               pattern=[[-1, P]], channel_multiplier=1).then_inc(const_made, 1)
            pool.affine_select(out=tri[:], in_=tri[:], compare_op=ALU.is_gt, fill=0.0, base=0,
                               pattern=[[1, P]], channel_multiplier=-1).then_inc(const_made, 1)
            pool.iota(pads_i[:, :, C_TOK], pattern=[[P, G + 1]], base=T, channel_multiplier=1).then_inc(const_made, 1)

            def power(k, src, dst):
                pool.wait_ge(var_ready, k + 1)
                pool.tensor_tensor(dst, src, mhalf[:], ALU.pow).then_inc(rstd_ready, 1)

            def scatter(r, k, par):
                pool.wait_ge(rstd_ready, k + 1)
                pool.wait_ge(pos_ready, r + 1)
                pool.sem_inc(scatter_open, 1)
                for t in range(TB):
                    pool.indirect_dma_start(sorted_rows, bass.IndirectOffsetOnAxis(ap=pos[:, par, t:t + 1], axis=0),
                                            stage[:, par, t, :], None).then_inc(scattered[par], 16)

            def scatter_pads(n):
                pool.wait_ge(tables_ready, n + 1)
                for g in range(G):
                    pool.indirect_dma_start(sorted_rows, bass.IndirectOffsetOnAxis(ap=pad_pos[:, g:g + 1], axis=0),
                                            pads[:, g, :], None).then_inc(pads_scattered, 16)

            def ffn(n, dst):
                def put(j):
                    pool.wait_ge(y_ready, j + (n * NS + 1) + OPEN)
                    pool.sem_inc(scatter_open, 1)
                    pool.indirect_dma_start(dst, bass.IndirectOffsetOnAxis(ap=yidx[:, 0:1], axis=0),
                                            yt[:], None).then_inc(y_scattered, 16)
                    pool.wait_ge(y_scattered, (j + (n * NS + 1)) * 16)
                    pool.sem_inc(y_free, 1)

                with pool.Fori(0, NS) as j:
                    put(j)

            pool.sem_inc(y_free, OPEN)
            power(0, ln_t[:, 5, :], stage[:, 0, :, C_RSTD])
            with pool.Fori(0, B // 2 - 1) as i:
                for par in range(2):
                    r = i * 2 + par
                    power(r + 1, ln_t[:, 5, :], stage[:, 1 - par, :, C_RSTD])
                    scatter(r, r, par)
            power(B - 1, ln_t[:, 5, :], stage[:, 1, :, C_RSTD])
            scatter(B - 2, B - 2, 0)
            scatter(B - 1, B - 1, 1)
            scatter_pads(0)
            ffn(0, mid)

            pool.memset(va[:], 0.0).then_inc(apads_made, 1)
            pool.memset(km[:], 0.0).then_inc(apads_made, 1)
            last_block = S // STRIDE - 1
            over = [(1 if k in (0, last_block) else 2) + (1 if k >= last_block - 1 else 0) for k in range(last_block + 1)]
            for n in range(NWIN):
                for half in range(2):
                    pool.wait_ge(*((icount_made, 2 * n + half) if n or half else (apads_made, 2)))
                    pool.memset(inv_count[half * STRIDE:(half + 1) * STRIDE, n:n + 1],
                                (2.0 if n == NWIN - 1 else 1.0) / over[n + half]).then_inc(icount_made, 1)
            pool.wait_ge(icount_made, 2 * NWIN)
            power(prep_use(0), ln_t[:, 5, :], ln_t[:, 4, :])
            pool.wait_ge(aw_loaded, 16 * ATTN_LOADS)

            def batch(b, first_, last):
                def accumulate(n):
                    pool.wait_ge(ct_ready, b * NWIN + (n + 1))
                    pool.wait_ge(acc_done if n else ctx_zero, b * NWIN + n if n else b + 1)
                    win = ctxt[:, :, n * STRIDE:n * STRIDE + W]
                    pool.tensor_tensor(win, win, ct[:, n % 2], ALU.add).then_inc(acc_done, 1)

                pool.wait_ge(o_done, b * TB + OPEN)
                pool.sem_inc(batch_open, 1)
                pool.memset(ctxt[:], 0.0).then_inc(ctx_zero, 1)
                if not first_:
                    power(route_use(b - 1), ln_t[:, 5, :], stage[:, 0, :, C_RSTD])
                accumulate(0)
                if not last:
                    power(prep_use(b + 1), ln_t[:, 5, :], ln_t[:, 4, :])
                accumulate(1)
                if not first_:
                    scatter(b + (B - 1), route_use(b - 1), 0)
                for n in range(2, NWIN):
                    accumulate(n)
                    if n == NWIN - 3:
                        pool.wait_ge(res_loaded, (b + 1) * 16)
                        pool.tensor_tensor(stage[:, 0, :, 0:D], stage[:, 0, :, 0:D],
                                           bo_s.unsqueeze(1).to_broadcast([P, TB, D]), ALU.add).then_inc(res_biased, 1)

            batch(0, True, False)
            with pool.Fori(1, B - 1) as b:
                batch(b, False, False)
            batch(B - 1, False, True)
            power(route_use(B - 1), ln_t[:, 5, :], stage[:, 0, :, C_RSTD])
            scatter(2 * B - 1, route_use(B - 1), 0)
            scatter_pads(1)
            ffn(1, out)

        @block.scalar
        def _(act):
            act.sem_inc(ht0_ready, OPEN)
            for e in range(NEXP):
                act.dma_start(wg[:, :, e, :], gate_w[e].rearrange("(c p) f -> p c f", p=P)).then_inc(w_loaded, 16)
                act.dma_start(wu[:, :, e, :], up_w[e].rearrange("(c p) f -> p c f", p=P)).then_inc(w_loaded, 16)
                act.dma_start(wd[:, :, e, :], down_w[e].rearrange("(c p) n -> p c n", p=P)).then_inc(w_loaded, 16)

            def copy_xnt(k):
                act.wait_ge(xnt_psum, k * DC + (1 + OPEN))
                nc.scalar.copy(xnt[:, 0, :], bank[6][:]).then_inc(xnt0_ready, 1)

            def exp_logits(r, lg):
                act.wait_ge(logits_done, r + 1)
                nc.scalar.activation(ex[:], lg[:, 0:TB * NR].rearrange("p (t r) -> p t r", r=NR),
                                     ACT.Exp, scale=-1.0).then_inc(ex_ready, 1)

            def ffn(n):
                t0 = n * NS

                def silu(j, e, first_=False):
                    act.wait_ge(gu_done, j * E + (t0 * E + e + 1))
                    if not first_:
                        act.wait_ge(h_ready, j * E + (t0 * E + e - 1))
                    nc.scalar.activation(sl[:, e], bank[2 * e][:], ACT.Silu).then_inc(silu_done, 1)

                def copy_xt(j):
                    act.wait_ge(xt_psum, j + (t0 + 1) + OPEN)
                    nc.scalar.copy(xt[:], bank[7][:, 0:D].rearrange("p (c t) -> p c t", c=DC)).then_inc(xt_ready, 1)

                def copy_ht(j):
                    act.wait_ge(ht_psum, j * E + (t0 * E + 1))
                    nc.scalar.copy(ht[:, 0], bank[4][:]).then_inc(ht0_ready, 1)

                nc.scalar.preload_act_table(ACT.Silu)
                copy_xt(0)
                silu(0, 0, True)
                silu(0, 1, True)
                copy_xt(1)
                copy_ht(0)
                with act.Fori(1, NS - 1) as j:
                    silu(j, 0)
                    silu(j, 1)
                    copy_xt(j + 1)
                    copy_ht(j)
                silu(NS - 1, 0)
                silu(NS - 1, 1)
                copy_ht(NS - 1)

            nc.scalar.preload_act_table(ACT.Exp)
            copy_xnt(0)
            with act.Fori(0, B - 1) as r:
                exp_logits(r, bank[2])
                copy_xnt(r + 1)
            exp_logits(B - 1, bank[2])
            ffn(0)

            nc.scalar.preload_act_table(ACT.Exp)
            act.wait_ge(aw_loaded, 16 * ATTN_LOADS)
            nc.scalar.mul(qkb[:, 2, :], qkb[:, 0, :], -1.0 / HD ** 0.5).then_inc(qb_ready, 1)
            act.wait_ge(qb_ready, 1)

            def copy_q(b):
                for m in range(DC):
                    act.wait_ge(proj_done, b * NPROJ + (DC + m + 1))
                    nc.scalar.activation(qt[:, m, :], bank[6 + m][:], ACT.Identity, bias=qkb[:, 2, m:m + 1],
                                         scale=-1.0 / HD ** 0.5).then_inc(q_ready, 1)

            def copy_values(b, n):
                act.wait_ge(pv_done, b * UNITS + (n + 1) * NQ)
                if n:
                    act.wait_ge(ct_ready, b * NWIN + n)
                nc.scalar.copy(vsum, bank[4][:, 0:DC * W]).then_inc(vsum_ready, 1)

            def batch(b, first_, last):
                for u in range(UNITS):
                    n, q = divmod(u, NQ)
                    act.wait_ge(sb_ready, b * UNITS + (u + 1))
                    if u >= NB:
                        act.wait_ge(pt_psum, b * UNITS + (u - NB + 1))
                    for h in range(HQ):
                        a = nc.scalar.activation(prob[:, u % NB, h], sbias[:, u % NB, h], ACT.Exp,
                                                 bias=nmax[:, u % NB, h:h + 1], scale=-1.0,
                                                 accum_out=rsum[:, n % 2, q * HQ + h:q * HQ + h + 1])
                    a.then_inc(p_ready, 1)
                    if q == 1 and n:
                        copy_values(b, n - 1)
                    for s in steps(u):
                        if s == "copy_route" and not first_:
                            copy_xnt(route_use(b - 1))
                        if s == "logits" and not first_:
                            exp_logits(b + (B - 1), bank[6])
                        if s == "copy_prep" and not last:
                            copy_xnt(prep_use(b + 1))
                copy_values(b, NWIN - 1)
                if not last:
                    copy_q(b + 1)

            copy_xnt(prep_use(0))
            copy_q(0)
            batch(0, True, False)
            with act.Fori(1, B - 1) as b:
                batch(b, False, False)
            batch(B - 1, False, True)
            copy_xnt(route_use(B - 1))
            exp_logits(2 * B - 1, bank[6])
            ffn(1)

        @block.tensor
        def _(pe):
            for s in (xnt_psum, xt_psum, s_done, o_done):
                pe.sem_inc(s, OPEN)

            def transpose(dst, src):
                return nc.tensor.transpose(dst, src, ident[:])

            def turn_batch(k):
                pe.wait_ge(xa_ready, k * TB + TB)
                for c in range(DC):
                    for t in range(TB):
                        tr = transpose(bank[6 + c][:, t * P:(t + 1) * P], xa[:, t, c * P:(c + 1) * P])
                    tr.then_inc(xnt_psum, 1)

            def logits(r, k, lg):
                pe.wait_ge(xnt0_ready, k + 1)
                pe.wait_ge(xnt1_ready, k + 1)
                for t in range(TB):
                    for c in range(DC):
                        mm = nc.tensor.matmul(lg[:, t * NR:(t + 1) * NR], xnt[:, c, t * P:(t + 1) * P], wr[:, c, :],
                                              start=(c == 0), stop=(c == DC - 1))
                mm.then_inc(logits_done, 1)

            def rank(r, rk):
                pe.wait_ge(oh_ready, r + 1)
                nc.tensor.matmul(rk[:, 0:TB * G], tri[:], oh[:].rearrange("p t g -> p (t g)"), start=True, stop=False)
                nc.tensor.matmul(rk[:, 0:TB * G], ones[:], seen[:, 0:TB].rearrange("p t g -> p (t g)"),
                                 start=False, stop=True).then_inc(rank_done, 1)

            def ffn(n, tot):
                t0 = n * NS
                nc.tensor.matmul(tot[:, 0:G], ones[:], seen[:, TB], start=True, stop=True).then_inc(totals_done, 1)

                def tx(j):
                    pe.wait_ge(xn_ready, j + (t0 + 1))
                    pe.wait_ge(xt_ready, j + t0)
                    for c in range(DC):
                        tr = transpose(bank[7][:, c * P:(c + 1) * P], xn[:, c * P:(c + 1) * P])
                    tr.then_inc(xt_psum, 1)

                def gate_up(j, g, e, first_=False):
                    pe.wait_ge(xt_ready, j + (t0 + 1))
                    if not first_:
                        pe.wait_ge(h_ready, j * E + (t0 * E + e - 1))
                    for bk_, w in ((bank[2 * e], wg), (bank[2 * e + 1], wu)):
                        for c in range(DC):
                            mm = nc.tensor.matmul(bk_[:], xt[:, c, :], flat(w[:, c, bass.ds(g * E + e, 1), :]),
                                                  start=(c == 0), stop=(c == DC - 1))
                    mm.then_inc(gu_done, 1)

                def th(j, e):
                    pe.wait_ge(h_ready, j * E + (t0 * E + e + 1))
                    pe.wait_ge((ht0_ready, ht1_ready)[e], j + t0 + OPEN)
                    for f in range(FC):
                        tr = transpose(bank[4 + e][:, f * P:(f + 1) * P], hb[:, e, f * P:(f + 1) * P])
                    tr.then_inc(ht_psum, 1)

                def down(j, g, e):
                    pe.wait_ge((ht0_ready, ht1_ready)[e], j + (t0 + 1) + OPEN)
                    if e == 0:
                        pe.wait_ge(y_ready, j + t0 + OPEN)
                    for f in range(FC):
                        mm = nc.tensor.matmul(bank[6][:, 0:D], ht[:, e, f * P:(f + 1) * P],
                                              flat(wd[:, f, bass.ds(g * E + e, 1), :]),
                                              start=(e == 0 and f == 0), stop=(e == E - 1 and f == FC - 1))
                    if e == E - 1:
                        mm.then_inc(d_done, 1)

                def group(j):
                    at_ = tile_group[0:1, j:j + 1] if type(j) is int else tile_group[0:1, bass.ds(j, 1)]
                    return pe.value_load(at_, min_val=0, max_val=G - 1)

                pe.wait_ge(tables_ready, n + 1)
                pe.wait_ge(w_loaded, 16 * 3 * NEXP)
                if n:
                    pe.wait_ge(w_reloaded, 16 * 2 * NEXP)
                tx(0)
                g0 = group(0)
                gate_up(0, g0, 0, first_=True)
                gate_up(0, g0, 1, first_=True)
                tx(1)
                th(0, 0)
                with pe.Fori(1, NS - 1) as j:
                    ga = group(j)
                    gb = group(j - 1)
                    gate_up(j, ga, 0)
                    th(j - 1, 1)
                    down(j - 1, gb, 0)
                    gate_up(j, ga, 1)
                    tx(j + 1)
                    th(j, 0)
                    down(j - 1, gb, 1)
                j = NS - 1
                ga, gb = group(j), group(j - 1)
                gate_up(j, ga, 0)
                th(j - 1, 1)
                down(j - 1, gb, 0)
                gate_up(j, ga, 1)
                th(j, 0)
                down(j - 1, gb, 1)
                th(j, 1)
                down(j, ga, 0)
                down(j, ga, 1)

            pe.wait_ge(const_made, CONSTS)
            pe.wait_ge(wr_loaded, 16 * (1 + G))
            turn_batch(0)
            with pe.Fori(0, B - 1) as r:
                logits(r, r, bank[2])
                turn_batch(r + 1)
                rank(r, bank[3])
            logits(B - 1, B - 1, bank[2])
            rank(B - 1, bank[3])
            ffn(0, bank[2])

            pe.wait_ge(aw_loaded, 16 * ATTN_LOADS)
            pe.wait_ge(apads_made, 2)

            def project_k(b, m):
                pe.wait_ge(xnt0_ready, prep_use(b) + 1)
                pe.wait_ge(xnt1_ready, prep_use(b) + 1)
                for c in range(DC):
                    mm = nc.tensor.matmul(bank[6 + m][:], wk_s[:, c, m * P:(m + 1) * P], xnt[:, c, :],
                                          start=(c == 0), stop=(c == DC - 1))
                mm.then_inc(proj_done, 1)

            def project_q(b):
                pe.wait_ge(k_ready, b * DC + DC)
                for m in range(DC):
                    for c in range(DC):
                        mm = nc.tensor.matmul(bank[6 + m][:], wq_s[:, c, m * P:(m + 1) * P], xnt[:, c, :],
                                              start=(c == 0), stop=(c == DC - 1))
                    mm.then_inc(proj_done, 1)

            def project_v(b):
                for t in range(TB):
                    if t < 2:
                        pe.wait_ge(q_ready, b * DC + (t + 1))
                    else:
                        pe.wait_ge(v_ready, b * TB + (t - 1))
                    for c in range(DC):
                        mm = nc.tensor.matmul(bank[6 + t % 2][:, 0:D], xnt[:, c, t * P:(t + 1) * P], wv_s[:, c, :],
                                              start=(c == 0), stop=(c == DC - 1))
                    mm.then_inc(proj_done, 1)

            def batch(b, first_, last):
                def scores(u):
                    n, q = divmod(u, NQ)
                    if u == 0:
                        pe.wait_ge(km_loaded, (b + 1) * (16 * H) + OPEN)
                        pe.wait_ge(q_ready, (b + 1) * DC)
                    if u >= 2:
                        pe.wait_ge(sb_ready, b * UNITS + (u - 1))
                    nc.tensor.matmul(bank[u % 2][:].rearrange("p (h k) -> p h k", h=HQ),
                                     qt[:, q * HQ // HC, n * STRIDE:n * STRIDE + W],
                                     km[:, q * HQ:(q + 1) * HQ, n * STRIDE:n * STRIDE + W],
                                     start=True, stop=True).then_inc(s_done, 1)

                def turn(u):
                    pe.wait_ge(p_ready, b * UNITS + (u + 1))
                    if u >= 2:
                        pe.wait_ge(pt_ready, b * UNITS + (u - 1))
                    for h in range(HQ):
                        tr = transpose(bank[2 + u % 2][:, h * W:(h + 1) * W], prob[:, u % NB, h])
                    tr.then_inc(pt_psum, 1)

                def values(u):
                    n, q = divmod(u, NQ)
                    if u == 0:
                        pe.wait_ge(v_ready, (b + 1) * TB)
                    if u == NQ:
                        pe.wait_ge(va_shifted, (b + 1) * (16 * SHIFTS))
                    if n and q == 0:
                        pe.wait_ge(vsum_ready, b * NWIN + n)
                    pe.wait_ge(pt_ready, b * UNITS + (u + 1))
                    for h in range(HQ):
                        m, pair = divmod((q * HQ + h) // 2, HC // 2)
                        mm = nc.tensor.matmul(bank[4][HS * pair:HS * (pair + 1), m * W:(m + 1) * W], va[:, n, q * HQ + h, :],
                                              pt_s[:, u % 2, h * W:(h + 1) * W], start=(h % 2 == 0), stop=(h % 2 == 1))
                    mm.then_inc(pv_done, 1)

                def factors(n):
                    pe.wait_ge(rexp_ready, b * NWIN + (n + 1))
                    if n:
                        pe.wait_ge(ct_ready, b * NWIN + n)
                    for m in range(DC):
                        mm = nc.tensor.matmul(bank[5][:, m * W:(m + 1) * W],
                                              rexp[:, m * HC:(m + 1) * HC, :].rearrange("p h i -> p (h i)"), ident[:],
                                              start=True, stop=True)
                    mm.then_inc(rb_done, 1)

                scores(0)
                scores(1)
                for u in range(UNITS):
                    if u + 2 < UNITS:
                        scores(u + 2)
                    turn(u)
                    if u:
                        values(u - 1)
                    if u % NQ == 1 and u > NQ:
                        factors(u // NQ - 1)
                    for s in steps(u):
                        if s == "turn_route" and not first_:
                            pe.wait_ge(res_ready, b * TB + OPEN)
                            turn_batch(route_use(b - 1))
                        if s == "logits" and not first_:
                            logits(b + (B - 1), route_use(b - 1), bank[6])
                        if s == "rank" and not first_:
                            rank(b + (B - 1), bank[7])
                        if s == "turn_prep" and not last:
                            if not first_:
                                pe.wait_ge(pos_ready, b + B)
                            turn_batch(prep_use(b + 1))
                        if s == "k0" and not last:
                            project_k(b + 1, 0)
                        if s == "k1" and not last:
                            project_k(b + 1, 1)
                values(UNITS - 1)
                factors(NWIN - 1)
                if not last:
                    project_q(b + 1)
                    project_v(b + 1)
                for t in range(TB):
                    if t >= 2:
                        pe.wait_ge(res_ready, b * TB + (t - 1) + OPEN)
                    elif not last:
                        pe.wait_ge(v_ready, (b + 1) * TB + TB - 1 + t)
                    if t == 0:
                        pe.wait_ge(acc_done, (b + 1) * NWIN)
                    for c in range(DC):
                        mm = nc.tensor.matmul(bank[6 + t % 2][:, 0:D], ctxt[:, c, t * P:(t + 1) * P], wo_s[:, c, :],
                                              start=(c == 0), stop=(c == DC - 1))
                    mm.then_inc(o_done, 1)

            turn_batch(prep_use(0))
            project_k(0, 0)
            project_k(0, 1)
            project_q(0)
            project_v(0)
            batch(0, True, False)
            with pe.Fori(1, B - 1) as b:
                batch(b, False, False)
            batch(B - 1, False, True)
            pe.wait_ge(res_ready, B * TB + OPEN)
            turn_batch(route_use(B - 1))
            logits(2 * B - 1, route_use(B - 1), bank[6])
            rank(2 * B - 1, bank[7])
            ffn(1, bank[6])

        @block.vector
        def _(dve):
            for s in (ht1_ready, y_ready, res_ready):
                dve.sem_inc(s, OPEN)

            class Chain:

                def __init__(self, name, start):
                    self.name, self.start, self.n = name, start, 0

                def __call__(self, ins):
                    self.n += 1
                    ins.then_inc(self.name, 1)
                    dve.wait_ge(self.name, self.start + self.n)

            def bc(v, axis, shape):
                return v.unsqueeze(axis).to_broadcast(shape)

            def norm_stats(k, src, mean):
                step = Chain(norm_step, k * NORM_STEPS)
                for t in range(TB):
                    i = nc.vector.bn_stats(stats[:, t, :], src[:, t, 0:D])
                step(i)
                s, d, v, dd, _, var = (ln_t[:, n, :] for n in range(6))
                nc.vector.tensor_tensor(s, stats[:, :, 1], stats[:, :, 4], ALU.add)
                nc.vector.tensor_tensor(d, stats[:, :, 1], stats[:, :, 4], ALU.subtract)
                step(nc.vector.tensor_tensor(v, stats[:, :, 2], stats[:, :, 5], ALU.add))
                nc.vector.tensor_scalar(mean, s, 0.5, None, ALU.mult)
                nc.vector.scalar_tensor_tensor(out=dd, in0=d, scalar=0.25, in1=d, op0=ALU.mult, op1=ALU.mult)
                step(nc.vector.tensor_scalar(v, v, 1.0 / D, LN_EPS, ALU.mult, ALU.add))
                assert step.n == NORM_STEPS
                nc.vector.tensor_tensor(var, v, dd, ALU.add).then_inc(var_ready, 1)

            def normalise(k, src, mean, rstd):
                dve.wait_ge(rstd_ready, k + 1)
                dve.wait_ge(xnt_psum, k * DC + OPEN)
                for t in range(TB):
                    nc.vector.tensor_scalar(xa[:, t, :], src[:, t, 0:D], mean[:, t:t + 1], rstd[:, t:t + 1],
                                            ALU.subtract, ALU.mult).then_inc(xa_ready, 1)

            def copy_xnt(k):
                dve.wait_ge(xnt_psum, k * DC + DC + OPEN)
                nc.vector.tensor_copy(xnt[:, 1, :], bank[7][:]).then_inc(xnt1_ready, 1)

            def stats_route(k, par, tile0):
                st = stage[:, par]
                tok = token_no[:, bass.ds(tile0, TB)] if type(tile0) is not int else token_no[:, tile0:tile0 + TB]
                nc.vector.tensor_copy(stage_i[:, par, :, C_TOK], tok)
                norm_stats(k, st, st[:, :, C_MEAN])

            def norm_route(k, par):
                st = stage[:, par]
                normalise(k, st, st[:, :, C_MEAN], st[:, :, C_RSTD])

            def choose(r, par):
                step = Chain(route_step, r * ROUTE_STEPS)
                dve.wait_ge(ex_ready, r + 1)
                step(nc.vector.tensor_scalar(ex[:], ex[:], 1.0, None, ALU.add))
                step(nc.vector.reciprocal(sg[:], ex[:]))
                step(nc.vector.tensor_reduce(best[:], sg[:, :, 0:G], AX.X, ALU.max))
                step(nc.vector.tensor_tensor(eq[:], sg[:, :, 0:G], bc(best[:], 2, [P, TB, G]), ALU.is_ge))
                step(nc.vector.tensor_tensor(eqw[:], eq[:], bc(gweight[:], 1, [P, TB, G]), ALU.mult))
                step(nc.vector.tensor_reduce(first[:], eqw[:], AX.X, ALU.max))
                nc.vector.tensor_tensor(oh[:], eqw[:], bc(first[:], 2, [P, TB, G]), ALU.is_equal)
                step(nc.vector.tensor_copy(seen[:, 0], seen[:, TB]))
                for t in range(TB):
                    i = nc.vector.tensor_tensor(seen[:, t + 1], seen[:, t], oh[:, t], ALU.add)
                    if t < TB - 1:
                        step(i)
                i.then_inc(oh_ready, 1)
                step(nc.vector.tensor_tensor(picked[:], sg[:, :, G:].rearrange("p t (g e) -> p t g e", g=G),
                                             bc(oh[:], 3, [P, TB, G, E]), ALU.mult))
                step(nc.vector.tensor_reduce(u01[:], picked[:].rearrange("p t g e -> p t e g"), AX.X, ALU.add))
                s, d, den, rc = (rs4[:, n, :] for n in range(4))
                nc.vector.tensor_scalar(d, best[:], TOPK_EPS, None, ALU.add)
                step(nc.vector.tensor_tensor(s, u01[:, :, 0], u01[:, :, 1], ALU.add))
                step(nc.vector.scalar_tensor_tensor(out=den, in0=s, scalar=TOPK_EPS, in1=d, op0=ALU.add, op1=ALU.mult))
                step(nc.vector.reciprocal(rc, den))
                step(nc.vector.tensor_tensor(s, best[:], rc, ALU.mult))
                step(nc.vector.tensor_tensor(stage[:, par, :, C_W:C_W + E], u01[:], bc(s, 2, [P, TB, E]), ALU.mult))
                return step

            def find_place(r, par, rk, step):
                dve.wait_ge(rank_done, r + 1)
                step(nc.vector.tensor_tensor(place[:], rk[:, 0:TB * G].rearrange("p (t g) -> p t g", g=G),
                                             bc(gcap[:], 1, [P, TB, G]), ALU.add))
                step(nc.vector.tensor_tensor(place[:], place[:], oh[:], ALU.mult))
                step(nc.vector.tensor_reduce(posf[:], place[:], AX.X, ALU.add))
                assert step.n == ROUTE_STEPS - 1, step.n
                step(nc.vector.tensor_copy(pos[:, par], posf[:]))
                dve.sem_inc(pos_ready, 1)

            def tables(n, tot):
                step = Chain(table_step, n * TABLE_STEPS)
                dve.wait_ge(totals_done, n + 1)
                step(nc.vector.tensor_scalar(tot_i[:, 0], tot[:, 0:G], float(P - 1), None, ALU.add))
                step(nc.vector.tensor_single_scalar(tot_i[:, 1], tot_i[:, 0], 7, ALU.arith_shift_right))
                nc.vector.memset(base[:, 0:1], 0.0)
                nc.vector.scalar_tensor_tensor(out=padf[:], in0=tot[:, 0:G], scalar=part_no[:], in1=gcap[:],
                                               op0=ALU.add, op1=ALU.add)
                step(nc.vector.tensor_copy(need[:], tot_i[:, 1]))
                nc.vector.tensor_copy(pad_pos[:], padf[:])
                nc.vector.tensor_scalar(jump[:], need[:], -float(P), float(CAP), ALU.mult, ALU.add)
                for g in range(G):
                    step(nc.vector.tensor_tensor(base[:, g + 1:g + 2], base[:, g:g + 1], need[:, g:g + 1], ALU.add))
                grp, row, a, c = (tt[:, i, :] for i in range(4))
                nc.vector.tensor_scalar(grp, tile_no[:], base[:, 1:2], None, ALU.is_ge)
                step(nc.vector.tensor_scalar(row, tile_no[:], float(P), None, ALU.mult))
                for g in range(1, G):
                    if g > 1:
                        nc.vector.tensor_scalar(a, tile_no[:], base[:, g:g + 1], None, ALU.is_ge)
                    step(nc.vector.tensor_scalar(c, tile_no[:], base[:, g:g + 1], jump[:, g - 1:g], ALU.is_ge, ALU.mult))
                    if g > 1:
                        nc.vector.tensor_tensor(grp, grp, a, ALU.add)
                    step(nc.vector.tensor_tensor(row, row, c, ALU.add))
                nc.vector.tensor_scalar(a, tile_no[:], base[:, G:G + 1], None, ALU.is_ge)
                step(nc.vector.tensor_scalar(c, row, -1.0, float(SPARE), ALU.mult, ALU.add))
                step(nc.vector.tensor_tensor(c, c, a, ALU.mult))
                step(nc.vector.tensor_tensor(row, row, c, ALU.add))
                nc.vector.tensor_copy(tile_group[:], grp)
                nc.vector.memset(seen[:, TB], 0.0)
                step(nc.vector.tensor_copy(tile_start[:], row))
                assert step.n == TABLE_STEPS, step.n
                dve.sem_inc(tables_ready, 1)

            def ffn(n):
                t0 = n * NS

                def of_tile(v, j, lo, hi):
                    if type(j) is int:
                        return v[:, j, lo:hi]
                    return flat(v[:, bass.ds(j, 1), lo:hi])

                def norm_tile(j):
                    dve.wait_ge(xs_loaded, (j + (t0 + 1)) * 16)
                    dve.wait_ge(xt_psum, j + t0 + OPEN)
                    nc.vector.tensor_scalar(xn[:], of_tile(tiles, j, 0, D), of_tile(tiles, j, C_MEAN, C_MEAN + 1),
                                            of_tile(tiles, j, C_RSTD, C_RSTD + 1), ALU.subtract, ALU.mult).then_inc(xn_ready, 1)

                def product(j, e, first_=False):
                    dve.wait_ge(silu_done, j * E + (t0 * E + e + 1))
                    if not first_:
                        dve.wait_ge(ht_psum, j * E + (t0 * E + e - 1))
                    nc.vector.scalar_tensor_tensor(out=hb[:, e], in0=bank[2 * e + 1][:], scalar=of_tile(tiles, j, C_W + e, C_W + e + 1),
                                                   in1=sl[:, e], op0=ALU.mult, op1=ALU.mult).then_inc(h_ready, 1)

                def copy_ht(j):
                    dve.wait_ge(ht_psum, j * E + (t0 * E + 2))
                    nc.vector.tensor_copy(ht[:, 1], bank[5][:]).then_inc(ht1_ready, 1)

                def finish(j):
                    dve.wait_ge(d_done, j + (t0 + 1))
                    dve.wait_ge(y_free, j + t0 + OPEN)
                    nc.vector.tensor_copy(yidx[:], of_tile(tiles_i, j, C_TOK, C_TOK + 1))
                    nc.vector.scalar_tensor_tensor(out=yt[:], in0=bank[6][:, 0:D], scalar=0.5, in1=of_tile(tiles, j, 0, D),
                                                   op0=ALU.mult, op1=ALU.add).then_inc(y_ready, 1)

                norm_tile(0)
                norm_tile(1)
                product(0, 0, first_=True)
                product(0, 1, first_=True)
                with dve.Fori(1, NS - 1) as j:
                    copy_ht(j - 1)
                    product(j, 0)
                    norm_tile(j + 1)
                    product(j, 1)
                    finish(j - 1)
                j = NS - 1
                copy_ht(j - 1)
                product(j, 0)
                product(j, 1)
                finish(j - 1)
                copy_ht(j)
                finish(j)

            dve.wait_ge(const_made, CONSTS)
            dve.wait_ge(x_loaded[0], 16)
            stats_route(0, 0, 0)
            norm_route(0, 0)
            copy_xnt(0)

            def route_two(i, last):
                for par in range(2):
                    r = i * 2 + par
                    if not (last and par):
                        dve.wait_ge(x_loaded[1 - par], (i + (1 + par)) * 16)
                        stats_route(r + 1, 1 - par, (r + 1) * TB)
                        norm_route(r + 1, 1 - par)
                    step = choose(r, par)
                    if not (last and par):
                        copy_xnt(r + 1)
                    find_place(r, par, bank[3], step)

            with dve.Fori(0, B // 2 - 1) as i:
                route_two(i, False)
            route_two(B // 2 - 1, True)
            tables(0, bank[2])
            ffn(0)

            dve.wait_ge(xb_loaded, 16)
            norm_stats(prep_use(0), xb, mean_b[:])
            normalise(prep_use(0), xb, mean_b[:], ln_t[:, 4, :])
            copy_xnt(prep_use(0))
            dve.wait_ge(aw_loaded, 16 * ATTN_LOADS)
            nc.vector.tensor_scalar(nbias[:], nbias[:], -1.0, None, ALU.mult).then_inc(nbias_ready, 1)
            dve.wait_ge(nbias_ready, 1)
            dve.wait_ge(icount_made, 2 * NWIN)

            def copy_k(b, m):
                dve.wait_ge(proj_done, b * NPROJ + (m + 1))
                if m == 0:
                    dve.wait_ge(km_loaded, b * (16 * H) + OPEN)
                nc.vector.tensor_scalar(kt[:, m, :], bank[6 + m][:], qkb[:, 1, m:m + 1], None, ALU.add).then_inc(k_ready, 1)

            def copy_v(b):
                def pairs(v):
                    return v.rearrange("p (a e i) -> p a e i", e=2, i=HD)

                for t in range(TB):
                    dve.wait_ge(proj_done, b * NPROJ + (2 * DC + t + 1))
                    dst = va[:, 2 * t].rearrange("p (a b) (f i) -> p a (b f) i", b=2, i=HD)[:, :, 0:4:3, :]
                    nc.vector.tensor_tensor(dst, pairs(bank[6 + t % 2][:, 0:D]), pairs(bv_s), ALU.add).then_inc(v_ready, 1)

            def batch(b, first_, last):
                def biased(u):
                    dve.wait_ge(s_done, b * UNITS + (u + 1) + OPEN)
                    if u >= NB:
                        dve.wait_ge(p_ready, b * UNITS + (u - NB + 1))
                    dve.sem_inc(unit_open, 1)
                    for h in range(HQ):
                        i = nc.vector.tensor_tensor_reduce(out=sbias[:, u % NB, h], in0=bank[u % 2][:, h * W:(h + 1) * W],
                                                           in1=nbias[:, (u % NQ) * HQ + h], scale=1.0, scalar=BIG,
                                                           op0=ALU.add, op1=ALU.min, accum_out=nmax[:, u % NB, h:h + 1])
                    i.then_inc(sb_ready, 1)

                def copy_pt(u):
                    dve.wait_ge(pt_psum, b * UNITS + (u + 1))
                    if u >= 2:
                        dve.wait_ge(pv_done, b * UNITS + (u - 1))
                    nc.vector.tensor_copy(pt_s[:, u % 2], bank[2 + u % 2][:]).then_inc(pt_ready, 1)

                def inverse(n):
                    dve.wait_ge(p_ready, b * UNITS + (n + 1) * NQ)
                    nc.vector.reciprocal(rinv, rsum[:, n % 2]).then_inc(rinv_ready, 1)
                    dve.wait_ge(rinv_ready, b * NWIN + (n + 1))
                    if n:
                        dve.wait_ge(rb_done, b * NWIN + n)
                    nc.vector.tensor_scalar(rexp[:], bc(rinv, 2, [P, H, HD]), inv_count[:, n:n + 1], None,
                                            ALU.mult).then_inc(rexp_ready, 1)

                def weigh(n):
                    dve.wait_ge(rb_done, b * NWIN + (n + 1))
                    dve.wait_ge(vsum_ready, b * NWIN + (n + 1))
                    if n >= 2:
                        dve.wait_ge(acc_done, b * NWIN + (n - 1))
                    nc.vector.tensor_tensor(ct[:, n % 2], bank[5][:, 0:DC * W].rearrange("p (c k) -> p c k", c=DC),
                                            vsum.rearrange("p (c k) -> p c k", c=DC), ALU.mult).then_inc(ct_ready, 1)

                biased(0)
                biased(1)
                step = None
                for u in range(UNITS):
                    if u + 2 < UNITS:
                        biased(u + 2)
                    copy_pt(u)
                    if u % NQ == 0 and u:
                        inverse(u // NQ - 1)
                    if u % NQ == 2 and u > NQ:
                        weigh(u // NQ - 1)
                    for s in steps(u):
                        if s == "stats_route" and not first_:
                            stats_route(route_use(b - 1), 0, (b - 1) * TB)
                        if s == "norm_route" and not first_:
                            norm_route(route_use(b - 1), 0)
                        if s == "copy_route" and not first_:
                            copy_xnt(route_use(b - 1))
                        if s == "choose" and not first_:
                            step = choose(b + (B - 1), 0)
                        if s == "place" and not first_:
                            find_place(b + (B - 1), 0, bank[7], step)
                        if s == "stats_prep" and not last:
                            dve.wait_ge(xb_loaded, (b + 2) * 16)
                            norm_stats(prep_use(b + 1), xb, mean_b[:])
                        if s == "norm_prep" and not last:
                            normalise(prep_use(b + 1), xb, mean_b[:], ln_t[:, 4, :])
                        if s == "copy_prep" and not last:
                            copy_xnt(prep_use(b + 1))
                        if s == "k0_copy" and not last:
                            copy_k(b + 1, 0)
                        if s == "k1_copy" and not last:
                            copy_k(b + 1, 1)
                inverse(NWIN - 1)
                weigh(NWIN - 1)
                if not last:
                    copy_v(b + 1)
                dve.wait_ge(res_biased, b + 1)
                for t in range(TB):
                    dve.wait_ge(o_done, b * TB + (t + 1) + OPEN)
                    nc.vector.tensor_tensor(stage[:, 0, t, 0:D], bank[6 + t % 2][:, 0:D], stage[:, 0, t, 0:D],
                                            ALU.add).then_inc(res_ready, 1)
                dve.wait_ge(res_ready, b * TB + TB + OPEN)

            copy_k(0, 0)
            copy_k(0, 1)
            copy_v(0)
            batch(0, True, False)
            with dve.Fori(1, B - 1) as b:
                batch(b, False, False)
            batch(B - 1, False, True)
            stats_route(route_use(B - 1), 0, (B - 1) * TB)
            norm_route(route_use(B - 1), 0)
            copy_xnt(route_use(B - 1))
            step = choose(2 * B - 1, 0)
            find_place(2 * B - 1, 0, bank[7], step)
            tables(1, bank[6])
            ffn(1)


_INS = ['L0_attn_hidden_states', 'L0_attn_Wq', 'L0_attn_bq', 'L0_attn_Wk', 'L0_attn_bk', 'L0_attn_Wv', 'L0_attn_bv',
        'L0_attn_Wo', 'L0_attn_bo', 'L0_attn_pos_bias', 'L0_ffn_macro_w', 'L0_ffn_micro_w', 'L0_ffn_gate_w',
        'L0_ffn_up_w', 'L0_ffn_down_w']


def kernel(**inputs):
    import numpy as _np
    import concourse.bacc as _bacc
    from concourse import mybir as _mybir
    from concourse.bass_utils import run_bass_kernel_spmd as _run

    nc = _bacc.Bacc("TRN2", target_bir_lowering=False, num_devices=1)
    arrays, args = {}, []
    for name in _INS:
        a = _np.ascontiguousarray(inputs[name])
        arrays[f"in_{name}"] = a
        args.append(nc.dram_tensor(f"in_{name}", a.shape, _mybir.dt.from_np(a.dtype), kind="ExternalInput").ap())
    args.append(nc.dram_tensor("out_0", (T + (G + 1) * P, D), F32, kind="ExternalOutput").ap())
    macaron_kernel(nc, *args)
    r = _run(nc, [arrays], core_ids=[0])
    return r.results[0]["out_0"][:T].reshape(B, S, D)
```

```python
import concourse.bass as bass
from concourse import mybir
from contextlib import ExitStack

F32 = mybir.dt.float32
I32 = mybir.dt.int32
F16 = mybir.dt.float16
ALU = mybir.AluOpType
ACT = mybir.ActivationFunctionType
AX = mybir.AxisListType

P = 128
B, S, D = 8, 512, 256
T = B * S
NT = T // P
TB = S // P
DC = D // P
F = 512
FC = F // P
G, E = 4, 2
NEXP = G * E
NS = NT + G - 1
NR = G + NEXP
C_W, C_MEAN, C_RSTD, C_TOK, RW = D, D + 2, D + 3, D + 4, D + 5
CAP = T + P
SPARE = G * CAP
H, HD = 16, 16
W, STRIDE = 128, 64
NWIN = (S - W) // STRIDE + 1
HQ = 4
NQ = H // HQ
UNITS = NWIN * NQ
HS = 2 * HD
NB = 4
HC = P // HD
LN_EPS = 1e-5
TOPK_EPS = 1e-9
BIG = 3.0e38
CH = DC * F
NGU = 2 * NEXP
NMAT = NGU + NEXP
AHEAD = 2
X_SCALE = 2.0 ** 11
W_SCALE = 2.0 ** 14
H_SCALE = 2.0 ** 15 / (X_SCALE * W_SCALE * (2 * D) ** 2)
WMIN = 1e-12
EXPONENT = 0x7F800000
SCALE_STEPS = 7
LOOK = (4, 5)
SPLIT = (6, 7)
OPEN = 1
NORM_STEPS, ROUTE_STEPS, TABLE_STEPS = 3, 21, 18
CONSTS = 6 + 2 * G + 3 + 3
V_BANK = (6, 6, 7, 6)
NPROJ = 2 * DC + TB
ATTN_LOADS = 9
SHIFTS = 2


def macaron_kernel(nc, x_in, Wq, bq, Wk, bk, Wv, bv, Wo, bo, pos_bias, macro_w, micro_w, gate_w, up_w, down_w, out):
    ctx = ExitStack()
    with ctx:
        def sb(name, shape, dt=F32):
            return ctx.enter_context(nc.sbuf_tensor(name, shape, dt))

        def sem(name):
            return ctx.enter_context(nc.semaphore(name))

        sorted_rows = nc.dram_tensor("sorted_rows", [SPARE + P, RW], F32, kind="Internal").ap()
        saved = nc.dram_tensor("saved", [NGU, P, 2 * CH], F16, kind="Internal").ap()
        mid = nc.dram_tensor("mid", [T + (G + 1) * P, D], F32, kind="Internal").ap()

        w_all = sb("w_all", [P, (NMAT + AHEAD) * CH])
        w16 = w_all[:, :].bitcast(F16)
        gu16 = w16[:, 0:NGU * 2 * CH].rearrange("p (e w h c f) -> p e w h c f", e=NEXP, w=2, h=2, c=DC)
        d16 = w16[:, NGU * 2 * CH:NMAT * 2 * CH].rearrange("p (e h c n) -> p e h c n", e=NEXP, h=2, c=FC)

        def w32(k):
            return w_all[:, (k + AHEAD) * CH:(k + AHEAD + 1) * CH]

        def w_part(k, h):
            return w16[:, (2 * k + h) * CH:(2 * k + h + 1) * CH]

        big = sb("big", [P, NS * RW])
        tiles = big[:, :].rearrange("p (t r) -> p t r", r=RW)
        tiles_i = big[:, :].bitcast(I32).rearrange("p (t r) -> p t r", r=RW)
        km = big[:, 0:H * S].rearrange("p (h s) -> p h s", h=H)

        ident = sb("ident", [P, P])
        tri = sb("tri", [P, P])
        ones = sb("ones", [P, P])
        mhalf = sb("mhalf", [P, TB])
        gweight = sb("gweight", [P, G])
        gcap = sb("gcap", [P, G])
        part_no = sb("part_no", [P, 1])
        tile_no = sb("tile_no", [P, NS])
        token_no = sb("token_no", [P, NT], I32)
        pads = sb("pads", [P, G + 1, RW])
        pads_i = pads[:].bitcast(I32)
        wr = sb("wr", [P, DC, NR])

        stage = sb("stage", [P, TB, RW])
        stage_i = stage[:].bitcast(I32)

        def rows_in(r, v):
            return v[:, bass.ds(r * TB, TB), :] if type(r) is not int else v[:, r * TB:(r + 1) * TB, :]

        stats = sb("stats", [P, TB, 6])
        ln_t = sb("ln_t", [P, 6, TB])
        mean_b = sb("mean_b", [P, TB])
        xa = sb("xa", [P, TB, D])
        xnt = sb("xnt", [P, DC, S])
        ex = sb("ex", [P, TB, NR])
        sg = sb("sg", [P, TB, NR])
        best = sb("best", [P, TB])
        eq = sb("eq", [P, TB, G])
        eqw = sb("eqw", [P, TB, G])
        first = sb("first", [P, TB])
        oh = sb("oh", [P, TB, G])
        seen = sb("seen", [P, TB + 1, G])
        picked = sb("picked", [P, TB, G, E])
        u01 = sb("u01", [P, TB, E])
        rs4 = sb("rs4", [P, 4, TB])
        place = sb("place", [P, TB, G])
        posf = sb("posf", [P, TB])
        pos = sb("pos", [P, B + 1, TB], I32)
        tot_i = sb("tot_i", [P, 2, G], I32)
        need = sb("need", [P, G])
        base = sb("base", [P, G + 1])
        jump = sb("jump", [P, G])
        padf = sb("padf", [P, G])
        pad_pos = sb("pad_pos", [P, G], I32)
        tt = sb("tt", [P, 4, NS])
        tile_group = sb("tile_group", [P, NS], I32)
        tile_start = sb("tile_start", [P, NS], I32)
        xn = sb("xn", [P, D])
        xt = sb("xt", [P, 2, DC, P], F16)
        sl = sb("sl", [P, E, F])
        hb = sb("hb", [P, E, F])
        ht = sb("ht", [P, E, 2, F], F16)
        ew = sb("ew", [P, E])
        wmax = sb("wmax", [P, NMAT])
        wm = sb("wm", [P, 3])
        wmt = sb("wmt", [3, 4])
        w_pow = sb("w_pow", [P, 3])
        w_inv = sb("w_inv", [P, 3])
        w_scale = sb("w_scale", [P, 3])
        back = sb("back", [P, 3])
        yt = sb("yt", [P, D])
        yidx = sb("yidx", [P, 1], I32)

        at = [0]

        def part(*shape):
            n = 1
            for k in shape:
                n *= k
            v = w_all[:, at[0]:at[0] + n]
            at[0] += n
            names = "abcd"[:len(shape)]
            if len(shape) > 1:
                v = v.rearrange(f"p ({' '.join(names)}) -> p {' '.join(names)}",
                                **{c: k for c, k in zip(names, shape)})
            return v

        nbias = part(H, W)
        wq_s, wk_s, wv_s = part(DC, D), part(DC, D), part(DC, D)
        bv_s = part(D)
        xb = part(TB, D)
        kt = part(DC, S)
        sbias = part(NB, HQ, W)
        prob = w_all[:, NMAT * CH:(NMAT + AHEAD) * CH].rearrange("p (u h k) -> p u h k", u=NB, h=HQ)
        qt = (part(DC, S), sb("qt1", [P, DC, S])[:])
        va = (part(NWIN, H, HS), sb("va1", [P, NWIN, H, HS])[:])
        pt_s = part(2, HQ * W)
        nmax = part(NB, HQ)
        rsum = part(2, H)
        rinv = part(H)
        rexp = part(H, HD)
        vsum = part(DC * W)
        qkb = part(3, DC)
        inv_count = part(NWIN)
        wo_s, bo_s = part(DC, D), part(D)
        assert NGU * CH >= at[0] and at[0] - DC * D - D >= NGU * CH * (G - 1) // G
        ct = sb("ct", [P, 2, DC, W])
        ctxt = (sb("ctxt0", [P, DC, S]), sb("ctxt1", [P, DC, S]))

        bank = [ctx.enter_context(nc.psum_tensor(f"bank{i}", [P, 512], F32)) for i in range(8)]

        xnt_r = sl

        const_made, spare_written = sem("const_made"), sem("spare_written")
        x_loaded = [sem("x_loaded0"), sem("x_loaded1")]
        wr_loaded, w_loaded, w_reloaded = sem("wr_loaded"), sem("w_loaded"), sem("w_reloaded")
        norm_step, var_ready, rstd_ready = sem("norm_step"), sem("var_ready"), sem("rstd_ready")
        xa_ready, xnt_psum, xnt_ready = sem("xa_ready"), sem("xnt_psum"), sem("xnt_ready")
        logits_done, ex_ready, route_step = sem("logits_done"), sem("ex_ready"), sem("route_step")
        oh_ready, rank_done, pos_ready = sem("oh_ready"), sem("rank_done"), sem("pos_ready")
        scattered = [sem("scattered1"), sem("scattered2")]
        totals_done, table_step, tables_ready, pads_scattered = (sem("totals_done"), sem("table_step"),
                                                                 sem("tables_ready"), sem("pads_scattered"))
        xs_loaded, xn_ready, xt_psum = sem("xs_loaded"), sem("xn_ready"), sem("xt_psum")
        xt_high, xt_ready, ew_ready = sem("xt_high"), sem("xt_ready"), sem("ew_ready")
        wmax_found, wmax_turned, wmax_diag, wmax_spread = (sem("wmax_found"), sem("wmax_turned"), sem("wmax_diag"),
                                                           sem("wmax_spread"))
        scale_step, scales_ready, w_high, w_low, w_saved = (sem("scale_step"), sem("scales_ready"), sem("w_high"),
                                                            sem("w_low"), sem("w_saved"))
        gu_done, silu_done, h_ready = sem("gu_done"), sem("silu_done"), sem("h_ready")
        ht_psum, ht_high, ht_ready = sem("ht_psum"), sem("ht_high"), sem("ht_ready")
        d_done, y_ready, y_scattered, y_free = sem("d_done"), sem("y_ready"), sem("y_scattered"), sem("y_free")
        aw_loaded, apads_made, nbias_ready, qb_ready, icount_made = (
            sem("aw_loaded"), sem("apads_made"), sem("nbias_ready"), sem("qb_ready"), sem("icount_made"))
        xb_loaded, res_loaded = sem("xb_loaded"), sem("res_loaded")
        proj_done, k_ready, q_ready, v_ready = sem("proj_done"), sem("k_ready"), sem("q_ready"), sem("v_ready")
        km_loaded = [sem("km_loaded0"), sem("km_loaded1")]
        s_done, sb_ready, p_ready = sem("s_done"), sem("sb_ready"), sem("p_ready")
        pt_psum, pt_ready, pv_done = sem("pt_psum"), sem("pt_ready"), sem("pv_done")
        rinv_ready, rexp_ready, rb_done, vsum_ready, ct_ready = (
            sem("rinv_ready"), sem("rexp_ready"), sem("rb_done"), sem("vsum_ready"), sem("ct_ready"))
        va_shifted, res_biased = sem("va_shifted"), sem("res_biased")
        stage_free, km_zero = sem("stage_free"), sem("km_zero")
        ctx_zero, acc_done, o_done, res_ready = sem("ctx_zero"), sem("acc_done"), sem("o_done"), sem("res_ready")
        batch_open, unit_open, scatter_open = sem("batch_open"), sem("unit_open"), sem("scatter_open")

        def prep_use(b):
            return b * 2 + (B - 2) if type(b) is not int or b > 1 else B + b

        def route_use(b):
            return b * 2 + (B + 3) if type(b) is not int or b < B - 2 else 2 * B + b

        def flat(v):
            return v.rearrange("p a d -> p (a d)")

        SIDE = {0: ("stats0",),
                1: ("stats1",),
                3: ("norm0",),
                4: ("norm1",),
                5: ("o0",),
                6: ("o1", "add0"),
                7: ("o2", "add1"),
                8: ("o3", "add2"),
                9: ("add3",),
                10: ("turn_prep", "copy_prep", "r_stats0"),
                11: ("r_stats1",),
                12: ("k0", "copy_k0"),
                13: ("k1", "r_norm0", "copy_k1"),
                14: ("r_norm1",),
                16: ("turn_route",),
                17: ("copy_route",),
                19: ("logits", "q0", "copy_q0"),
                20: ("q1", "copy_q1"),
                21: ("choose0",),
                22: ("choose1", "v0"),
                23: ("rank", "copy_v0"),
                24: ("choose2", "v1"),
                25: ("choose3", "place", "copy_v1"),
                26: ("v2",),
                27: ("v3", "copy_v2", "copy_v3")}
        SIDE_LAST = {5: ("o0",), 6: ("o1", "add0"), 7: ("o2", "add1"), 8: ("o3", "add2"), 9: ("add3",), 10: ("r_stats0",),
                     11: ("r_stats1",), 13: ("r_norm0",), 14: ("r_norm1",), 15: ("turn_route",), 16: ("copy_route",),
                     18: ("logits",), 19: ("choose0",), 20: ("choose1",), 21: ("rank", "choose2"),
                     22: ("choose3", "place")}
        PREP = ("stats0", "stats1", "norm0", "norm1", "turn_prep", "copy_prep", "k0", "k1", "copy_k0",
                "copy_k1", "q0", "q1", "copy_q0", "copy_q1", "v0", "v1", "v2", "v3",
                "copy_v0", "copy_v1", "copy_v2", "copy_v3")

        def steps(u, first_, last):
            return [s for s in (SIDE_LAST if last else SIDE).get(u, ()) if not (last if s in PREP else first_)]

        def ahead(b, u, last):
            if u + 2 < UNITS:
                return b, u + 2
            return None if last else (b + 1, u + 2 - UNITS)

        def two_by_two(eng, batch):
            batch(0, 0, True, False)
            with eng.Fori(1, B // 2) as i:
                batch(i * 2 - 1, 1, False, False)
                batch(i * 2, 0, False, False)
            batch(B - 1, 1, False, True)

        def which(k):
            return 2 if k >= NGU else k % 2

        def beside(r):
            of = LOOK if r in LOOK else SPLIT
            n = NMAT // len(of)
            k = of.index(r) * n
            return range(k, k + n // 3), range(k + n // 3, k + n)

        block = ctx.enter_context(nc.Block())

        @block.sync
        def _(sp):
            for s in km_loaded:
                sp.sem_inc(s, OPEN)

            def load_x(r, par):
                sp.dma_start(rows_in(r, tiles)[:, :, 0:D], x_in[bass.ds(r, 1)].rearrange("a (t p) d -> p (a t) d", p=P)
                             if type(r) is not int else x_in[r].rearrange("(t p) d -> p t d", p=P)).then_inc(x_loaded[par], 16)

            load_x(0, 0)
            load_x(1, 1)
            sp.dma_start(wr[:, :, 0:G], macro_w.rearrange("(c p) g -> p c g", p=P)).then_inc(wr_loaded, 16)
            for g in range(G):
                sp.dma_start(wr[:, :, G + E * g:G + E * g + E],
                             micro_w[g].rearrange("(c p) e -> p c e", p=P)).then_inc(wr_loaded, 16)
            with sp.Fori(1, B // 2) as i:
                for par in range(2):
                    sp.wait_ge(x_loaded[par], i * 16)
                    load_x(i * 2 + par, par)
            for e in range(NEXP):
                for k, w, chunks in ((2 * e, gate_w, DC), (2 * e + 1, up_w, DC), (NGU + e, down_w, FC)):
                    sp.dma_start(w32(k).rearrange("p (c n) -> p c n", c=chunks),
                                  w[e].rearrange("(c p) n -> p c n", p=P)).then_inc(w_loaded, 16)
            sp.wait_ge(const_made, CONSTS)
            sp.dma_start(sorted_rows[SPARE:SPARE + P, :], pads[:, G, :]).then_inc(spare_written, 16)
            sp.dma_start(mid[T:T + (G + 1) * P, :].rearrange("(g p) d -> p g d", p=P), pads[:, :, 0:D]).then_inc(spare_written, 16)

            def ffn(n):
                t0 = n * NS
                sp.wait_ge(tables_ready, n + 1)
                sp.wait_ge(spare_written, 32)
                sp.wait_ge(scattered[n], 16 * TB * B)
                sp.wait_ge(pads_scattered, 16 * G * (n + 1))

                def load(j):
                    at_ = tile_start[0:1, bass.ds(j, 1)] if type(j) is not int else tile_start[0:1, j:j + 1]
                    row = sp.value_load(at_, min_val=0, max_val=SPARE)
                    dst = tiles[:, j, :] if type(j) is int else flat(tiles[:, bass.ds(j, 1), :])
                    sp.dma_start(dst, sorted_rows[bass.ds(row, P), :]).then_inc(xs_loaded, 16)

                def load_after(j):
                    sp.wait_ge(xs_loaded, (j + t0) * 16)
                    load(j)

                load(0)
                if n == 0:
                    sp.wait_ge(w_low, NMAT)
                    with sp.Fori(1, NGU + 1) as j:
                        load_after(j)
                        k = j - 1
                        sp.dma_start(saved[bass.ds(k, 1)].rearrange("a p n -> p (a n)"),
                                     w16[:, bass.ds(k * (2 * CH), 2 * CH)]).then_inc(w_saved, 16)
                with sp.Fori(1 if n else NGU + 1, NS) as j:
                    load_after(j)

            ffn(0)
            sp.wait_ge(d_done, NS)
            sp.wait_ge(w_saved, 16 * NGU)
            sp.dma_start(wq_s, Wq.rearrange("(c p) n -> p c n", p=P)).then_inc(aw_loaded, 16)
            sp.dma_start(wk_s, Wk.rearrange("(c p) n -> p c n", p=P)).then_inc(aw_loaded, 16)
            sp.dma_start(wv_s, Wv.rearrange("(c p) n -> p c n", p=P)).then_inc(aw_loaded, 16)
            sp.dma_start(nbias, pos_bias.rearrange("h q k -> q h k")).then_inc(aw_loaded, 16)
            sp.dma_start(bv_s, bv.partition_broadcast(P)).then_inc(aw_loaded, 16)
            sp.dma_start(qkb[:, 0, :], bq.rearrange("(c p) -> p c", p=P), allow_slow_non_contiguous=True).then_inc(aw_loaded, 16)
            sp.dma_start(qkb[:, 1, :], bk.rearrange("(c p) -> p c", p=P), allow_slow_non_contiguous=True).then_inc(aw_loaded, 16)
            sp.dma_start(wo_s, Wo.rearrange("(c p) n -> p c n", p=P)).then_inc(aw_loaded, 16)
            sp.dma_start(bo_s, bo.partition_broadcast(P)).then_inc(aw_loaded, 16)

            def rows_of(b):
                if type(b) is int:
                    return mid[b * S:(b + 1) * S, :].rearrange("(t p) d -> p t d", p=P)
                return mid[bass.ds(b * S, S), :].rearrange("(t p) d -> p t d", p=P)

            def load_batch(b):
                sp.dma_start(xb, rows_of(b)).then_inc(xb_loaded, 16)

            def mask_keys(b, half):
                cols = slice(half * S // 2, (half + 1) * S // 2)
                km2 = km.rearrange("p (c h) s -> p c h s", c=DC)
                for h in range(HC):
                    r = HD * h
                    sp.dma_start(km2[r:r + HD, :, h, cols], kt[r:r + HD, :, cols]).then_inc(km_loaded[half], 16)

            def shift_values(b, par):
                sp.wait_ge(v_ready, b * TB + TB)
                v = va[par]
                sp.dma_start(v[0:STRIDE, 1:NWIN:2], v[STRIDE:W, 0:NWIN - 1:2]).then_inc(va_shifted, 16)
                sp.dma_start(v[STRIDE:W, 1:NWIN:2], v[0:STRIDE, 2:NWIN:2]).then_inc(va_shifted, 16)

            def batch(b, par, first_, last):
                if not first_:
                    sp.wait_ge(stage_free, b - 1 + OPEN)
                    sp.dma_start(stage[:, :, 0:D], rows_of(b - 1)).then_inc(res_loaded, 16)
                if not last:
                    sp.wait_ge(k_ready, b * DC + 2 * DC)
                    sp.wait_ge(s_done, b * UNITS + 4 * NQ + OPEN)
                    mask_keys(b + 1, 0)
                    sp.wait_ge(xa_ready, (prep_use(b + 1) + 1) * TB)
                    load_batch(b + 2)
                    shift_values(b + 1, 1 - par)
                    sp.wait_ge(s_done, b * UNITS + UNITS + OPEN)
                    mask_keys(b + 1, 1)

            sp.wait_ge(y_scattered, 16 * NS)
            load_batch(0)
            sp.wait_ge(k_ready, DC)
            load_batch(1)
            sp.wait_ge(apads_made, 3)
            sp.wait_ge(km_zero, 1)
            mask_keys(0, 0)
            mask_keys(0, 1)
            shift_values(0, 0)
            two_by_two(sp, batch)
            sp.wait_ge(stage_free, B - 1 + OPEN)
            sp.dma_start(stage[:, :, 0:D], rows_of(B - 1)).then_inc(res_loaded, 16)
            sp.wait_ge(acc_done, B * NWIN)
            per = NGU // G
            for g in range(G):
                if g == G - 1:
                    sp.wait_ge(res_ready, B * TB + OPEN)
                sp.dma_start(w16[:, g * per * 2 * CH:(g + 1) * per * 2 * CH].rearrange("p (k n) -> p k n", k=per),
                             saved[g * per:(g + 1) * per].rearrange("k p n -> p k n")).then_inc(w_reloaded, 16)
            ffn(1)
            sp.wait_ge(y_scattered, 16 * NS * 2)

        @block.gpsimd
        def _(pool):
            for v, c in ((ident, 0.0), (tri, 1.0), (ones, 1.0), (mhalf, -0.5), (pads, 0.0), (seen, 0.0)):
                pool.memset(v[:], c).then_inc(const_made, 1)
            for g in range(G):
                pool.memset(gweight[:, g:g + 1], float(G - g)).then_inc(const_made, 1)
                pool.memset(gcap[:, g:g + 1], float(g * CAP)).then_inc(const_made, 1)
            pool.iota(tile_no[:], pattern=[[1, NS]], base=0, channel_multiplier=0,
                      allow_small_or_imprecise_dtypes=True).then_inc(const_made, 1)
            pool.iota(part_no[:], pattern=[[1, 1]], base=0, channel_multiplier=1,
                      allow_small_or_imprecise_dtypes=True).then_inc(const_made, 1)
            pool.iota(token_no[:], pattern=[[P, NT]], base=0, channel_multiplier=1).then_inc(const_made, 1)
            pool.wait_ge(const_made, 6 + 2 * G + 3)
            pool.affine_select(out=ident[:], in_=ident[:], compare_op=ALU.not_equal, fill=1.0, base=0,
                               pattern=[[-1, P]], channel_multiplier=1).then_inc(const_made, 1)
            pool.affine_select(out=tri[:], in_=tri[:], compare_op=ALU.is_gt, fill=0.0, base=0,
                               pattern=[[1, P]], channel_multiplier=-1).then_inc(const_made, 1)
            pool.iota(pads_i[:, :, C_TOK], pattern=[[P, G + 1]], base=T, channel_multiplier=1).then_inc(const_made, 1)

            def power(k, src, dst):
                pool.wait_ge(var_ready, k + 1)
                pool.tensor_tensor(dst, src, mhalf[:], ALU.pow).then_inc(rstd_ready, 1)

            def scatter(r, k, rows, place_no, counted):
                pool.wait_ge(rstd_ready, k + 1)
                pool.wait_ge(pos_ready, r + 1)
                pool.sem_inc(scatter_open, 1)
                for t in range(TB):
                    pool.indirect_dma_start(sorted_rows, bass.IndirectOffsetOnAxis(ap=pos[:, place_no, t:t + 1], axis=0),
                                            rows[:, t, :], None).then_inc(counted, 16)

            def scatter_pads(n):
                pool.wait_ge(tables_ready, n + 1)
                for g in range(G):
                    pool.indirect_dma_start(sorted_rows, bass.IndirectOffsetOnAxis(ap=pad_pos[:, g:g + 1], axis=0),
                                            pads[:, g, :], None).then_inc(pads_scattered, 16)

            def ffn(n, dst):
                def put(j):
                    pool.wait_ge(y_ready, j + (n * NS + 1) + OPEN)
                    pool.sem_inc(scatter_open, 1)
                    pool.indirect_dma_start(dst, bass.IndirectOffsetOnAxis(ap=yidx[:, 0:1], axis=0),
                                            yt[:], None).then_inc(y_scattered, 16)
                    pool.wait_ge(y_scattered, (j + (n * NS + 1)) * 16)
                    pool.sem_inc(y_free, 1)

                with pool.Fori(0, NS) as j:
                    put(j)

            pool.memset(va[1], 0.0).then_inc(apads_made, 1)

            pool.sem_inc(y_free, OPEN)
            pool.sem_inc(stage_free, OPEN)
            power(0, ln_t[:, 5, :], rows_in(0, tiles)[:, :, C_RSTD])
            for r in range(B):
                if r < B - 1:
                    power(r + 1, ln_t[:, 5, :], rows_in(r + 1, tiles)[:, :, C_RSTD])
                scatter(r, r, rows_in(r, tiles), r, scattered[0])
            scatter_pads(0)
            pool.wait_ge(spare_written, 32)
            ffn(0, mid)

            pool.wait_ge(w_saved, 16 * NGU)
            pool.memset(va[0], 0.0).then_inc(apads_made, 1)
            pool.memset(km[:, H // 2:], 0.0).then_inc(apads_made, 1)
            power(prep_use(0), ln_t[:, 5, :], ln_t[:, 4, :])
            last_block = S // STRIDE - 1
            over = [(1 if k in (0, last_block) else 2) + (1 if k >= last_block - 1 else 0) for k in range(last_block + 1)]
            for n in range(NWIN):
                for half in range(2):
                    pool.wait_ge(*((icount_made, 2 * n + half) if n or half else (apads_made, 3)))
                    pool.memset(inv_count[half * STRIDE:(half + 1) * STRIDE, n:n + 1],
                                (2.0 if n == NWIN - 1 else 1.0) / over[n + half]).then_inc(icount_made, 1)
            pool.wait_ge(icount_made, 2 * NWIN)
            pool.wait_ge(aw_loaded, 16 * ATTN_LOADS)

            def accumulate(b, par, n):
                pool.wait_ge(ct_ready, b * NWIN + (n + 1))
                pool.wait_ge(acc_done if n else ctx_zero, b * NWIN + n if n else b + 1)
                win = ctxt[par][:, :, n * STRIDE:n * STRIDE + W]
                pool.tensor_tensor(win, win, ct[:, (par + n) % 2], ALU.add).then_inc(acc_done, 1)

            def bias_residual(b):
                pool.wait_ge(res_loaded, (b + 1) * 16)
                pool.tensor_tensor(stage[:, :, 0:D], stage[:, :, 0:D],
                                   bo_s.unsqueeze(1).to_broadcast([P, TB, D]), ALU.add).then_inc(res_biased, 1)

            def batch(b, par, first_, last):
                if not last:
                    power(prep_use(b + 1), ln_t[:, 5, :], ln_t[:, 4, :])
                if not first_:
                    pool.wait_ge(o_done, (b - 1) * TB + OPEN)
                    pool.sem_inc(batch_open, 1)
                pool.memset(ctxt[par][:], 0.0).then_inc(ctx_zero, 1)
                if not first_:
                    accumulate(b - 1, 1 - par, NWIN - 1)
                    bias_residual(b - 1)
                for n in range(NWIN - 1):
                    accumulate(b, par, n)
                    if n == 1 and not first_:
                        power(route_use(b - 1), ln_t[:, 5, :], stage[:, :, C_RSTD])
                    if n == (3 if last else 4) and not first_:
                        scatter(b + (B - 1), route_use(b - 1), stage, B, scattered[1])
                if not first_:
                    pool.wait_ge(scattered[1], b * (16 * TB))
                    pool.sem_inc(stage_free, 1)

            two_by_two(pool, batch)
            bias_residual(B - 1)
            accumulate(B - 1, 1, NWIN - 1)
            power(route_use(B - 1), ln_t[:, 5, :], stage[:, :, C_RSTD])
            scatter(2 * B - 1, route_use(B - 1), stage, B, scattered[1])
            scatter_pads(1)
            ffn(1, out)

        @block.scalar
        def _(act):
            def high(k):
                if k >= AHEAD:
                    act.wait_ge(w_low, k - AHEAD + 1)
                i = which(k)
                nc.scalar.activation(w_part(k, 0), w32(k), ACT.Copy, scale=w_scale[:, i:i + 1]).then_inc(w_high, 1)

            def copy_xnt(k, dst=xnt):
                for c in range(DC):
                    act.wait_ge(xnt_psum, k * DC + (c + 1 + OPEN))
                    nc.scalar.copy(dst[:, c, :], bank[6 + c][:]).then_inc(xnt_ready, 1)

            def exp_logits(r, lg):
                act.wait_ge(logits_done, r + 1)
                nc.scalar.activation(ex[:], lg[:, 0:TB * NR].rearrange("p (t r) -> p t r", r=NR),
                                     ACT.Exp, scale=-1.0).then_inc(ex_ready, 1)

            def ffn(n):
                t0 = n * NS

                def silu(j, e, first_=False):
                    act.wait_ge(gu_done, j * E + (t0 * E + e + 1))
                    if not first_:
                        act.wait_ge(h_ready, j * E + (t0 * E + e - 1))
                    nc.scalar.activation(sl[:, e], bank[2 * e][:], ACT.Silu, scale=back[:, 0:1]).then_inc(silu_done, 1)

                def high_xt(j):
                    act.wait_ge(xt_psum, j + (t0 + 1) + OPEN)
                    nc.scalar.activation(xt[:, 0], bank[7][:, 0:D].rearrange("p (c t) -> p c t", c=DC), ACT.Copy,
                                         scale=X_SCALE).then_inc(xt_high, 1)

                def high_ht(j, e):
                    act.wait_ge(ht_psum, j * E + (t0 * E + e + 1))
                    nc.scalar.copy(ht[:, e, 0], bank[4 + e][:]).then_inc(ht_high, 1)

                nc.scalar.preload_act_table(ACT.Silu)
                high_xt(0)
                silu(0, 0, True)
                high_xt(1)
                silu(0, 1, True)
                high_ht(0, 0)
                with act.Fori(1, NS - 1) as j:
                    silu(j, 0)
                    high_ht(j - 1, 1)
                    high_xt(j + 1)
                    silu(j, 1)
                    high_ht(j, 0)
                j = NS - 1
                silu(j, 0)
                high_ht(j - 1, 1)
                silu(j, 1)
                high_ht(j, 0)
                high_ht(j, 1)

            nc.scalar.preload_act_table(ACT.Exp)
            copy_xnt(0)
            with act.Fori(0, SPLIT[0]) as r:
                exp_logits(r, bank[2])
                copy_xnt(r + 1)
            act.wait_ge(scales_ready, 1)
            for r in SPLIT:
                now, later = beside(r)
                for k in now:
                    high(k)
                exp_logits(r, bank[2])
                if r < B - 1:
                    copy_xnt(r + 1)
                for k in later:
                    high(k)
            ffn(0)

            nc.scalar.preload_act_table(ACT.Exp)
            act.wait_ge(aw_loaded, 16 * ATTN_LOADS)
            nc.scalar.mul(qkb[:, 2, :], qkb[:, 0, :], -1.0 / HD ** 0.5).then_inc(qb_ready, 1)
            act.wait_ge(qb_ready, 1)

            def copy_k(b, m):
                act.wait_ge(proj_done, b * NPROJ + (m + 1))
                if m == 0:
                    act.wait_ge(km_loaded[1], b * (16 * HC) + OPEN)
                nc.scalar.activation(kt[:, m, :], bank[6 + m][:], ACT.Identity, bias=qkb[:, 1, m:m + 1]).then_inc(k_ready, 1)

            def copy_q(b, par, m):
                act.wait_ge(proj_done, b * NPROJ + (DC + m + 1))
                nc.scalar.activation(qt[par][:, m, :], bank[6 + m][:], ACT.Identity, bias=qkb[:, 2, m:m + 1],
                                     scale=-1.0 / HD ** 0.5).then_inc(q_ready, 1)

            def copy_values(b, par, n):
                act.wait_ge(pv_done, b * UNITS + (n + 1) * NQ)
                if n or type(b) is not int or b:
                    act.wait_ge(ct_ready, b * NWIN + n)
                nc.scalar.copy(vsum, bank[4 + (par + n) % 2][:, 0:DC * W]).then_inc(vsum_ready, 1)

            def batch(b, par, first_, last):
                for u in range(UNITS):
                    n, q = divmod(u, NQ)
                    act.wait_ge(sb_ready, b * UNITS + (u + 1))
                    if u >= NB or not first_:
                        act.wait_ge(pt_psum, b * UNITS + (u - NB + 1))
                    for h in range(HQ):
                        a = nc.scalar.activation(prob[:, u % NB, h], sbias[:, u % NB, h], ACT.Exp,
                                                 bias=nmax[:, u % NB, h:h + 1], scale=-1.0,
                                                 accum_out=rsum[:, (par + n) % 2, q * HQ + h:q * HQ + h + 1])
                    a.then_inc(p_ready, 1)
                    if q == 2:
                        if n:
                            copy_values(b, par, n - 1)
                        elif not first_:
                            copy_values(b - 1, 1 - par, NWIN - 1)
                    for s in steps(u - 2, first_, last):
                        if s == "copy_route":
                            copy_xnt(route_use(b - 1), xnt_r)
                        if s == "logits":
                            exp_logits(b + (B - 1), bank[7])
                        if s == "copy_prep":
                            copy_xnt(prep_use(b + 1))
                        if s in ("copy_k0", "copy_k1"):
                            copy_k(b + 1, int(s[-1]))
                        if s in ("copy_q0", "copy_q1"):
                            copy_q(b + 1, 1 - par, int(s[-1]))

            copy_xnt(prep_use(0))
            copy_k(0, 0)
            copy_k(0, 1)
            copy_q(0, 0, 0)
            copy_q(0, 0, 1)
            two_by_two(act, batch)
            copy_values(B - 1, 1, NWIN - 1)
            copy_xnt(route_use(B - 1), xnt_r)
            exp_logits(2 * B - 1, bank[7])
            ffn(1)

        @block.tensor
        def _(pe):
            for s in (xnt_psum, xt_psum, s_done, o_done):
                pe.sem_inc(s, OPEN)

            def transpose(dst, src):
                return nc.tensor.transpose(dst, src, ident[:])

            def turn_batch(k):
                pe.wait_ge(xa_ready, k * TB + TB)
                for c in range(DC):
                    for t in range(TB):
                        tr = transpose(bank[6 + c][:, t * P:(t + 1) * P], xa[:, t, c * P:(c + 1) * P])
                    tr.then_inc(xnt_psum, 1)

            def logits(r, k, lg, src=xnt):
                pe.wait_ge(xnt_ready, k * DC + DC)
                for t in range(TB):
                    for c in range(DC):
                        mm = nc.tensor.matmul(lg[:, t * NR:(t + 1) * NR], src[:, c, t * P:(t + 1) * P], wr[:, c, :],
                                              start=(c == 0), stop=(c == DC - 1))
                mm.then_inc(logits_done, 1)

            def rank(r, rk):
                pe.wait_ge(oh_ready, r + 1)
                nc.tensor.matmul(rk[:, 0:TB * G], tri[:], oh[:].rearrange("p t g -> p (t g)"), start=True, stop=False)
                nc.tensor.matmul(rk[:, 0:TB * G], ones[:], seen[:, 0:TB].rearrange("p t g -> p (t g)"),
                                 start=False, stop=True).then_inc(rank_done, 1)

            def ffn(n, tot):
                t0 = n * NS
                nc.tensor.matmul(tot[:, 0:G], ones[:], seen[:, TB], start=True, stop=True).then_inc(totals_done, 1)

                def tx(j):
                    pe.wait_ge(xn_ready, j + (t0 + 1))
                    pe.wait_ge(xt_ready, j + t0)
                    for c in range(DC):
                        tr = transpose(bank[7][:, c * P:(c + 1) * P], xn[:, c * P:(c + 1) * P])
                    tr.then_inc(xt_psum, 1)

                def parts(chunks):
                    return [(hl, hr, c) for hl, hr in ((0, 0), (0, 1), (1, 0)) for c in range(chunks)]

                def gate_up(j, g, e, first_=False):
                    pe.wait_ge(xt_ready, j + (t0 + 1))
                    if not first_:
                        pe.wait_ge(h_ready, j * E + (t0 * E + e - 1))
                    for w in range(2):
                        for i, (hx, hw, c) in enumerate(parts(DC)):
                            mm = nc.tensor.matmul(bank[2 * e + w][:], xt[:, hx, c, :],
                                                  flat(gu16[:, bass.ds(g * E + e, 1), w, hw, c, :]),
                                                  start=(i == 0), stop=(i == 3 * DC - 1))
                    mm.then_inc(gu_done, 1)

                def th(j, e):
                    pe.wait_ge(h_ready, j * E + (t0 * E + e + 1))
                    pe.wait_ge(ht_ready, j * E + (t0 * E + e - 1) + OPEN)
                    for f in range(FC):
                        tr = transpose(bank[4 + e][:, f * P:(f + 1) * P], hb[:, e, f * P:(f + 1) * P])
                    tr.then_inc(ht_psum, 1)

                def down(j, g, e):
                    pe.wait_ge(ht_ready, j * E + (t0 * E + e + 1) + OPEN)
                    if e == 0:
                        pe.wait_ge(y_ready, j + t0 + OPEN)
                    for i, (hh, hw, f) in enumerate(parts(FC)):
                        mm = nc.tensor.matmul(bank[6][:, 0:D], ht[:, e, hh, f * P:(f + 1) * P],
                                              flat(d16[:, bass.ds(g * E + e, 1), hw, f, :]),
                                              start=(e == 0 and i == 0), stop=(e == E - 1 and i == 3 * FC - 1))
                    if e == E - 1:
                        mm.then_inc(d_done, 1)

                def group(j):
                    at_ = tile_group[0:1, j:j + 1] if type(j) is int else tile_group[0:1, bass.ds(j, 1)]
                    return pe.value_load(at_, min_val=0, max_val=G - 1)

                pe.wait_ge(tables_ready, n + 1)
                pe.wait_ge(w_low, NMAT)
                if n:
                    pe.wait_ge(w_reloaded, 16 * G)
                tx(0)
                g0 = group(0)
                gate_up(0, g0, 0, first_=True)
                gate_up(0, g0, 1, first_=True)
                tx(1)
                th(0, 0)
                with pe.Fori(1, NS - 1) as j:
                    ga = group(j)
                    gb = group(j - 1)
                    gate_up(j, ga, 0)
                    th(j - 1, 1)
                    down(j - 1, gb, 0)
                    gate_up(j, ga, 1)
                    tx(j + 1)
                    th(j, 0)
                    down(j - 1, gb, 1)
                j = NS - 1
                ga, gb = group(j), group(j - 1)
                gate_up(j, ga, 0)
                th(j - 1, 1)
                down(j - 1, gb, 0)
                gate_up(j, ga, 1)
                th(j, 0)
                down(j - 1, gb, 1)
                th(j, 1)
                down(j, ga, 0)
                down(j, ga, 1)

            pe.wait_ge(const_made, CONSTS)
            pe.wait_ge(wr_loaded, 16 * (1 + G))
            turn_batch(0)
            with pe.Fori(0, SPLIT[0]) as r:
                logits(r, r, bank[2])
                turn_batch(r + 1)
                rank(r, bank[3])
            pe.wait_ge(wmax_found, 1)
            nc.tensor.transpose(bank[4][0:3, 0:P], wm[:], ident[:]).then_inc(wmax_turned, 1)
            pe.wait_ge(wmax_diag, 1)
            nc.tensor.matmul(bank[5][:, 0:3], ones[0:3, :], wmt[:, 1:4], start=True, stop=True).then_inc(wmax_spread, 1)
            with pe.Fori(SPLIT[0], B - 1) as r:
                logits(r, r, bank[2])
                turn_batch(r + 1)
                rank(r, bank[3])
            logits(B - 1, B - 1, bank[2])
            rank(B - 1, bank[3])
            ffn(0, bank[2])

            pe.wait_ge(aw_loaded, 16 * ATTN_LOADS)
            pe.wait_ge(apads_made, 3)

            def project(m, w):
                for c in range(DC):
                    mm = nc.tensor.matmul(bank[6 + m][:], w[:, c, m * P:(m + 1) * P], xnt[:, c, :],
                                          start=(c == 0), stop=(c == DC - 1))
                mm.then_inc(proj_done, 1)

            def project_v(b, t, ranked):
                if t in (0, 2):
                    pe.wait_ge(q_ready, b * DC + (t // 2 + 1))
                else:
                    pe.wait_ge(v_ready, b * TB + (1 if t == 1 else 2))
                if t == 2 and ranked is not None:
                    pe.wait_ge(pos_ready, ranked)
                for c in range(DC):
                    mm = nc.tensor.matmul(bank[V_BANK[t]][:, 0:D], xnt[:, c, t * P:(t + 1) * P], wv_s[:, c, :],
                                          start=(c == 0), stop=(c == DC - 1))
                mm.then_inc(proj_done, 1)

            def project_out(b, par, t, ready=None):
                if t == 0:
                    pe.wait_ge(acc_done, (b + 1) * NWIN)
                if ready:
                    pe.wait_ge(*ready)
                if t >= 2:
                    pe.wait_ge(res_ready, b * TB + (t - 1) + OPEN)
                for c in range(DC):
                    mm = nc.tensor.matmul(bank[6 + t % 2][:, 0:D], ctxt[par][:, c, t * P:(t + 1) * P], wo_s[:, c, :],
                                          start=(c == 0), stop=(c == DC - 1))
                mm.then_inc(o_done, 1)

            def scores(b, par, u, early):
                n, q = divmod(u, NQ)
                if u == 0:
                    pe.wait_ge(km_loaded[0], (b + 1) * (16 * HC) + OPEN)
                    pe.wait_ge(q_ready, (b + 1) * DC)
                if u == 3 * NQ:
                    pe.wait_ge(km_loaded[1], (b + 1) * (16 * HC) + OPEN)
                if not early:
                    pe.wait_ge(sb_ready, b * UNITS + (u - 1))
                nc.tensor.matmul(bank[u % 2][:].rearrange("p (h k) -> p h k", h=HQ),
                                 qt[par][:, q * HQ // HC, n * STRIDE:n * STRIDE + W],
                                 km[:, q * HQ:(q + 1) * HQ, n * STRIDE:n * STRIDE + W],
                                 start=True, stop=True).then_inc(s_done, 1)

            def turn(b, u, early):
                pe.wait_ge(p_ready, b * UNITS + (u + 1))
                if not early:
                    pe.wait_ge(pt_ready, b * UNITS + (u - 1))
                for h in range(HQ):
                    tr = transpose(bank[2 + u % 2][:, h * W:(h + 1) * W], prob[:, u % NB, h])
                tr.then_inc(pt_psum, 1)

            def values(b, par, u, first_):
                n, q = divmod(u, NQ)
                if u == 0:
                    pe.wait_ge(v_ready, (b + 1) * TB)
                if u == NQ:
                    pe.wait_ge(va_shifted, (b + 1) * (16 * SHIFTS))
                if q == 0 and (n >= 2 or not first_):
                    pe.wait_ge(ct_ready, b * NWIN + (n - 1))
                pe.wait_ge(pt_ready, b * UNITS + (u + 1))
                for h in range(HQ):
                    m, pair = divmod((q * HQ + h) // 2, HC // 2)
                    mm = nc.tensor.matmul(bank[4 + (par + n) % 2][HS * pair:HS * (pair + 1), m * W:(m + 1) * W],
                                          va[par][:, n, q * HQ + h, :], pt_s[:, u % 2, h * W:(h + 1) * W],
                                          start=(h % 2 == 0), stop=(h % 2 == 1))
                mm.then_inc(pv_done, 1)

            def factors(b, par, n):
                pe.wait_ge(rexp_ready, b * NWIN + (n + 1))
                pe.wait_ge(vsum_ready, b * NWIN + (n + 1))
                for m in range(DC):
                    mm = nc.tensor.matmul(bank[4 + (par + n) % 2][:, (DC + m) * W:(DC + m + 1) * W],
                                          rexp[:, m * HC:(m + 1) * HC, :].rearrange("p h i -> p (h i)"), ident[:],
                                          start=True, stop=True)
                mm.then_inc(rb_done, 1)

            def batch(b, par, first_, last):
                for u in range(UNITS):
                    if ahead(b, u, last):
                        b2, u2 = ahead(b, u, last)
                        scores(b2, par if u2 > u else 1 - par, u2, False)
                    turn(b, u, first_ and u < 2)
                    if u:
                        values(b, par, u - 1, first_)
                    elif not first_:
                        values(b - 1, 1 - par, UNITS - 1, False)
                    if u % NQ == 2:
                        if u > NQ:
                            factors(b, par, u // NQ - 1)
                        elif not first_:
                            factors(b - 1, 1 - par, NWIN - 1)
                    for s in steps(u, first_, last):
                        if s == "turn_prep":
                            if not first_:
                                pe.wait_ge(res_ready, b * TB + OPEN)
                            turn_batch(prep_use(b + 1))
                        if s in ("k0", "k1"):
                            pe.wait_ge(xnt_ready, prep_use(b + 1) * DC + DC)
                            project(int(s[1]), wk_s)
                        if s in ("q0", "q1"):
                            m = int(s[1])
                            pe.wait_ge(k_ready, b * DC + (DC + m + 1))
                            if not first_:
                                if m == 0:
                                    pe.wait_ge(xnt_ready, route_use(b - 1) * DC + DC)
                                else:
                                    pe.wait_ge(ex_ready, b + B)
                            project(m, wq_s)
                        if s in ("v0", "v1", "v2", "v3"):
                            project_v(b + 1, int(s[1]), None if first_ else b + B)
                        if s in ("o0", "o1", "o2", "o3"):
                            t = int(s[1])
                            project_out(b - 1, 1 - par, t, (v_ready, b * TB + TB) if t < 2 else None)
                        if s == "turn_route":
                            pe.wait_ge(res_ready, b * TB + OPEN)
                            if not last:
                                pe.wait_ge(k_ready, b * DC + 2 * DC)
                            turn_batch(route_use(b - 1))
                        if s == "logits":
                            logits(b + (B - 1), route_use(b - 1), bank[7], xnt_r)
                        if s == "rank":
                            if not last:
                                pe.wait_ge(q_ready, b * DC + (DC + 2))
                            rank(b + (B - 1), bank[7])

            turn_batch(prep_use(0))
            pe.wait_ge(xnt_ready, prep_use(0) * DC + DC)
            for m in range(DC):
                project(m, wk_s)
            for m in range(DC):
                pe.wait_ge(k_ready, m + 1)
                project(m, wq_s)
            for t in range(TB):
                project_v(0, t, None)
            pe.wait_ge(v_ready, TB)
            scores(0, 0, 0, True)
            scores(0, 0, 1, True)
            two_by_two(pe, batch)
            values(B - 1, 1, UNITS - 1, False)
            factors(B - 1, 1, NWIN - 1)
            for t in range(TB):
                project_out(B - 1, 1, t, (xnt_ready, route_use(B - 2) * DC + DC) if t < 2 else None)
            pe.wait_ge(res_ready, B * TB + OPEN)
            turn_batch(route_use(B - 1))
            logits(2 * B - 1, route_use(B - 1), bank[7], xnt_r)
            rank(2 * B - 1, bank[6])
            ffn(1, bank[7])

        @block.vector
        def _(dve):
            for s in (ht_ready, y_ready, res_ready):
                dve.sem_inc(s, OPEN)

            class Chain:

                def __init__(self, name, start):
                    self.name, self.start, self.n = name, start, 0

                def __call__(self, ins):
                    self.n += 1
                    ins.then_inc(self.name, 1)
                    dve.wait_ge(self.name, self.start + self.n)

            def bc(v, axis, shape):
                return v.unsqueeze(axis).to_broadcast(shape)

            def whole(parts):
                said = None
                for said in parts:
                    pass
                return said

            def norm_stats(k, src, mean):
                step = Chain(norm_step, k * NORM_STEPS)
                for t in range(TB):
                    if t == TB // 2:
                        yield
                    i = nc.vector.bn_stats(stats[:, t, :], src[:, t, 0:D])
                step(i)
                s, d, v, dd, _, var = (ln_t[:, n, :] for n in range(6))
                nc.vector.tensor_tensor(s, stats[:, :, 1], stats[:, :, 4], ALU.add)
                nc.vector.tensor_tensor(d, stats[:, :, 1], stats[:, :, 4], ALU.subtract)
                step(nc.vector.tensor_tensor(v, stats[:, :, 2], stats[:, :, 5], ALU.add))
                nc.vector.tensor_scalar(mean, s, 0.5, None, ALU.mult)
                nc.vector.scalar_tensor_tensor(out=dd, in0=d, scalar=0.25, in1=d, op0=ALU.mult, op1=ALU.mult)
                step(nc.vector.tensor_scalar(v, v, 1.0 / D, LN_EPS, ALU.mult, ALU.add))
                assert step.n == NORM_STEPS
                nc.vector.tensor_tensor(var, v, dd, ALU.add).then_inc(var_ready, 1)

            def normalise(k, src, mean, rstd, half=None):
                dve.wait_ge(rstd_ready, k + 1)
                dve.wait_ge(xnt_psum, k * DC + OPEN)
                for t in range(TB) if half is None else range(half * TB // 2, (half + 1) * TB // 2):
                    nc.vector.tensor_scalar(xa[:, t, :], src[:, t, 0:D], mean[:, t:t + 1], rstd[:, t:t + 1],
                                            ALU.subtract, ALU.mult).then_inc(xa_ready, 1)

            def stats_route(k, st, st_i, tile0):
                tok = token_no[:, bass.ds(tile0, TB)] if type(tile0) is not int else token_no[:, tile0:tile0 + TB]
                nc.vector.tensor_copy(st_i[:, :, C_TOK], tok)
                yield from norm_stats(k, st, st[:, :, C_MEAN])

            def norm_route(k, st, half=None):
                normalise(k, st, st[:, :, C_MEAN], st[:, :, C_RSTD], half)

            def choose(r, rows):
                step = Chain(route_step, r * ROUTE_STEPS)
                dve.wait_ge(ex_ready, r + 1)
                step(nc.vector.tensor_scalar(ex[:], ex[:], 1.0, None, ALU.add))
                step(nc.vector.reciprocal(sg[:], ex[:]))
                step(nc.vector.tensor_reduce(best[:], sg[:, :, 0:G], AX.X, ALU.max))
                step(nc.vector.tensor_tensor(eq[:], sg[:, :, 0:G], bc(best[:], 2, [P, TB, G]), ALU.is_ge))
                yield step
                step(nc.vector.tensor_tensor(eqw[:], eq[:], bc(gweight[:], 1, [P, TB, G]), ALU.mult))
                step(nc.vector.tensor_reduce(first[:], eqw[:], AX.X, ALU.max))
                nc.vector.tensor_tensor(oh[:], eqw[:], bc(first[:], 2, [P, TB, G]), ALU.is_equal)
                step(nc.vector.tensor_copy(seen[:, 0], seen[:, TB]))
                for t in range(TB):
                    i = nc.vector.tensor_tensor(seen[:, t + 1], seen[:, t], oh[:, t], ALU.add)
                    if t < TB - 1:
                        step(i)
                i.then_inc(oh_ready, 1)
                yield step
                step(nc.vector.tensor_tensor(picked[:], sg[:, :, G:].rearrange("p t (g e) -> p t g e", g=G),
                                             bc(oh[:], 3, [P, TB, G, E]), ALU.mult))
                step(nc.vector.tensor_reduce(u01[:], picked[:].rearrange("p t g e -> p t e g"), AX.X, ALU.add))
                s, d, den, rc = (rs4[:, n, :] for n in range(4))
                nc.vector.tensor_scalar(d, best[:], TOPK_EPS, None, ALU.add)
                step(nc.vector.tensor_tensor(s, u01[:, :, 0], u01[:, :, 1], ALU.add))
                yield step
                step(nc.vector.scalar_tensor_tensor(out=den, in0=s, scalar=TOPK_EPS, in1=d, op0=ALU.add, op1=ALU.mult))
                step(nc.vector.reciprocal(rc, den))
                step(nc.vector.tensor_tensor(s, best[:], rc, ALU.mult))
                step(nc.vector.tensor_tensor(rows[:, :, C_W:C_W + E], u01[:], bc(s, 2, [P, TB, E]), ALU.mult))
                yield step

            def find_place(r, place_no, rk, step):
                dve.wait_ge(rank_done, r + 1)
                step(nc.vector.tensor_tensor(place[:], rk[:, 0:TB * G].rearrange("p (t g) -> p t g", g=G),
                                             bc(gcap[:], 1, [P, TB, G]), ALU.add))
                step(nc.vector.tensor_tensor(place[:], place[:], oh[:], ALU.mult))
                step(nc.vector.tensor_reduce(posf[:], place[:], AX.X, ALU.add))
                assert step.n == ROUTE_STEPS - 1, step.n
                dst = pos[:, place_no] if type(place_no) is int else flat(pos[:, bass.ds(place_no, 1)])
                step(nc.vector.tensor_copy(dst, posf[:]))
                dve.sem_inc(pos_ready, 1)

            def tables(n, tot):
                step = Chain(table_step, n * TABLE_STEPS)
                dve.wait_ge(totals_done, n + 1)
                step(nc.vector.tensor_scalar(tot_i[:, 0], tot[:, 0:G], float(P - 1), None, ALU.add))
                step(nc.vector.tensor_single_scalar(tot_i[:, 1], tot_i[:, 0], 7, ALU.arith_shift_right))
                nc.vector.memset(base[:, 0:1], 0.0)
                nc.vector.scalar_tensor_tensor(out=padf[:], in0=tot[:, 0:G], scalar=part_no[:], in1=gcap[:],
                                               op0=ALU.add, op1=ALU.add)
                step(nc.vector.tensor_copy(need[:], tot_i[:, 1]))
                nc.vector.tensor_copy(pad_pos[:], padf[:])
                nc.vector.tensor_scalar(jump[:], need[:], -float(P), float(CAP), ALU.mult, ALU.add)
                for g in range(G):
                    step(nc.vector.tensor_tensor(base[:, g + 1:g + 2], base[:, g:g + 1], need[:, g:g + 1], ALU.add))
                grp, row, a, c = (tt[:, i, :] for i in range(4))
                nc.vector.tensor_scalar(grp, tile_no[:], base[:, 1:2], None, ALU.is_ge)
                step(nc.vector.tensor_scalar(row, tile_no[:], float(P), None, ALU.mult))
                for g in range(1, G):
                    if g > 1:
                        nc.vector.tensor_scalar(a, tile_no[:], base[:, g:g + 1], None, ALU.is_ge)
                    step(nc.vector.tensor_scalar(c, tile_no[:], base[:, g:g + 1], jump[:, g - 1:g], ALU.is_ge, ALU.mult))
                    if g > 1:
                        nc.vector.tensor_tensor(grp, grp, a, ALU.add)
                    step(nc.vector.tensor_tensor(row, row, c, ALU.add))
                nc.vector.tensor_scalar(a, tile_no[:], base[:, G:G + 1], None, ALU.is_ge)
                step(nc.vector.tensor_scalar(c, row, -1.0, float(SPARE), ALU.mult, ALU.add))
                step(nc.vector.tensor_tensor(c, c, a, ALU.mult))
                step(nc.vector.tensor_tensor(row, row, c, ALU.add))
                nc.vector.tensor_copy(tile_group[:], grp)
                nc.vector.memset(seen[:, TB], 0.0)
                step(nc.vector.tensor_copy(tile_start[:], row))
                assert step.n == TABLE_STEPS, step.n
                dve.sem_inc(tables_ready, 1)

            def ffn(n):
                t0 = n * NS

                def of_tile(v, j, lo, hi):
                    if type(j) is int:
                        return v[:, j, lo:hi]
                    return flat(v[:, bass.ds(j, 1), lo:hi])

                def norm_tile(j):
                    dve.wait_ge(xs_loaded, (j + (t0 + 1)) * 16)
                    dve.wait_ge(xt_psum, j + t0 + OPEN)
                    nc.vector.tensor_scalar(xn[:], of_tile(tiles, j, 0, D), of_tile(tiles, j, C_MEAN, C_MEAN + 1),
                                            of_tile(tiles, j, C_RSTD, C_RSTD + 1), ALU.subtract, ALU.mult).then_inc(xn_ready, 1)

                def product(j, e, first_=False):
                    dve.wait_ge(silu_done, j * E + (t0 * E + e + 1))
                    if not first_:
                        dve.wait_ge(ht_psum, j * E + (t0 * E + e - 1))
                    if e == 0:
                        dve.wait_ge(ew_ready, j + (t0 + 1))
                    nc.vector.scalar_tensor_tensor(out=hb[:, e], in0=bank[2 * e + 1][:], scalar=ew[:, e:e + 1],
                                                   in1=sl[:, e], op0=ALU.mult, op1=ALU.mult).then_inc(h_ready, 1)

                def expert_weights(j, first_=False):
                    if not first_:
                        dve.wait_ge(h_ready, j * E + t0 * E)
                    nc.vector.tensor_scalar(ew[:], of_tile(tiles, j, C_W, C_W + E), back[:, 1:2], None,
                                            ALU.mult).then_inc(ew_ready, 1)

                def low_xt(j):
                    dve.wait_ge(xt_high, j + (t0 + 1))
                    nc.vector.scalar_tensor_tensor(out=xt[:, 1], in0=bank[7][:, 0:D].rearrange("p (c t) -> p c t", c=DC),
                                                   scalar=X_SCALE, in1=xt[:, 0], op0=ALU.mult,
                                                   op1=ALU.subtract).then_inc(xt_ready, 1)

                def low_ht(j, e):
                    dve.wait_ge(ht_high, j * E + (t0 * E + e + 1))
                    nc.vector.tensor_tensor(ht[:, e, 1], bank[4 + e][:], ht[:, e, 0], ALU.subtract).then_inc(ht_ready, 1)

                def finish(j):
                    dve.wait_ge(d_done, j + (t0 + 1))
                    dve.wait_ge(y_free, j + t0 + OPEN)
                    nc.vector.tensor_copy(yidx[:], of_tile(tiles_i, j, C_TOK, C_TOK + 1))
                    nc.vector.scalar_tensor_tensor(out=yt[:], in0=bank[6][:, 0:D], scalar=back[:, 2:3], in1=of_tile(tiles, j, 0, D),
                                                   op0=ALU.mult, op1=ALU.add).then_inc(y_ready, 1)

                norm_tile(0)
                expert_weights(0, first_=True)
                low_xt(0)
                norm_tile(1)
                product(0, 0, first_=True)
                low_xt(1)
                product(0, 1, first_=True)
                low_ht(0, 0)
                expert_weights(1)
                with dve.Fori(1, NS - 1) as j:
                    product(j, 0)
                    low_ht(j - 1, 1)
                    norm_tile(j + 1)
                    low_xt(j + 1)
                    product(j, 1)
                    low_ht(j, 0)
                    expert_weights(j + 1)
                    finish(j - 1)
                j = NS - 1
                product(j, 0)
                low_ht(j - 1, 1)
                product(j, 1)
                low_ht(j, 0)
                finish(j - 1)
                low_ht(j, 1)
                finish(j)

            dve.wait_ge(const_made, CONSTS)
            dve.wait_ge(x_loaded[0], 16)
            whole(stats_route(0, rows_in(0, tiles), rows_in(0, tiles_i), 0))
            norm_route(0, rows_in(0, tiles))

            def largest(k):
                nc.vector.tensor_reduce(wmax[:, k:k + 1], w32(k), AX.X, ALU.max, apply_absolute_value=True)

            def scales():
                step = Chain(scale_step, 0)
                nc.vector.tensor_reduce(wm[:, 0:2], wmax[:, 0:NGU].rearrange("p (e w) -> p w e", w=2), AX.X, ALU.max)
                nc.vector.tensor_reduce(wm[:, 2:3], wmax[:, NGU:NMAT], AX.X, ALU.max).then_inc(wmax_found, 1)
                dve.wait_ge(wmax_turned, 1)
                step(nc.vector.tensor_reduce(wmt[:, 0:1], bank[4][0:3, 0:P], AX.X, ALU.max))
                nc.vector.tensor_scalar(wmt[:, 1:4], ident[0:3, 0:3], wmt[:, 0:1], None, ALU.mult).then_inc(wmax_diag, 1)
                dve.wait_ge(wmax_spread, 1)
                step(nc.vector.tensor_scalar(wm[:], bank[5][:, 0:3], WMIN, None, ALU.max))
                step(nc.vector.tensor_single_scalar(w_pow[:].bitcast(I32), wm[:].bitcast(I32), EXPONENT, ALU.bitwise_and))
                step(nc.vector.reciprocal(w_inv[:], w_pow[:]))
                nc.vector.tensor_scalar(w_scale[:], w_inv[:], W_SCALE, None, ALU.mult)
                nc.vector.tensor_scalar(back[:, 0:1], w_pow[:, 0:1], 1.0 / (X_SCALE * W_SCALE), None, ALU.mult)
                step(nc.vector.tensor_scalar(back[:, 1:2], w_inv[:, 0:1], H_SCALE, None, ALU.mult))
                step(nc.vector.tensor_scalar(back[:, 2:3], w_pow[:, 0:1], w_pow[:, 1:2],
                                             0.5 / (X_SCALE * W_SCALE * H_SCALE * W_SCALE), ALU.mult, ALU.mult))
                step(nc.vector.tensor_tensor(back[:, 2:3], back[:, 2:3], w_pow[:, 2:3], ALU.mult))
                assert step.n == SCALE_STEPS, step.n
                dve.sem_inc(scales_ready, 1)

            def low(k):
                dve.wait_ge(w_high, k + 1)
                i = which(k)
                nc.vector.scalar_tensor_tensor(out=w_part(k, 1), in0=w32(k), scalar=w_scale[:, i:i + 1],
                                               in1=w_part(k, 0), op0=ALU.mult, op1=ALU.subtract).then_inc(w_low, 1)

            def route(r, x_count, between=None):
                now, later = beside(r) if between else ((), ())
                for k in now:
                    between(k)
                more = type(r) is not int or r < B - 1
                if more:
                    dve.wait_ge(*x_count)
                    whole(stats_route(r + 1, rows_in(r + 1, tiles), rows_in(r + 1, tiles_i), (r + 1) * TB))
                    norm_route(r + 1, rows_in(r + 1, tiles))
                step = whole(choose(r, rows_in(r, tiles)))
                if not more:
                    find_place(r, r, bank[3], step)
                    tables(0, bank[2])
                for k in later:
                    between(k)
                if more:
                    find_place(r, r, bank[3], step)

            def came(r):
                return x_loaded[r % 2], 16 * (r // 2 + 1)

            for r in range(LOOK[0]):
                route(r, came(r + 1))
            dve.wait_ge(w_loaded, 16 * NMAT)
            for r in LOOK:
                route(r, came(r + 1), largest)
            scales()
            for r in SPLIT:
                route(r, came(r + 1), low)
            ffn(0)

            dve.wait_ge(y_ready, NS + OPEN)
            nc.vector.memset(km[:, 0:H // 2], 0.0).then_inc(km_zero, 1)
            dve.wait_ge(xb_loaded, 16)
            whole(norm_stats(prep_use(0), xb, mean_b[:]))
            normalise(prep_use(0), xb, mean_b[:], ln_t[:, 4, :])
            dve.wait_ge(aw_loaded, 16 * ATTN_LOADS)
            nc.vector.tensor_scalar(nbias[:], nbias[:], -1.0, None, ALU.mult).then_inc(nbias_ready, 1)
            dve.wait_ge(nbias_ready, 1)
            dve.wait_ge(icount_made, 2 * NWIN)

            def copy_v(b, par, t):
                def pairs(v):
                    return v.rearrange("p (a e i) -> p a e i", e=2, i=HD)

                dve.wait_ge(proj_done, b * NPROJ + (2 * DC + t + 1))
                dst = va[par][:, 2 * t].rearrange("p (a b) (f i) -> p a (b f) i", b=2, i=HD)[:, :, 0:4:3, :]
                nc.vector.tensor_tensor(dst, pairs(bank[V_BANK[t]][:, 0:D]), pairs(bv_s), ALU.add).then_inc(v_ready, 1)

            def biased(b, u, early=False):
                dve.wait_ge(s_done, b * UNITS + (u + 1) + OPEN)
                if not early:
                    dve.wait_ge(p_ready, b * UNITS + (u - NB + 1))
                dve.sem_inc(unit_open, 1)
                for h in range(HQ):
                    i = nc.vector.tensor_tensor_reduce(out=sbias[:, u % NB, h], in0=bank[u % 2][:, h * W:(h + 1) * W],
                                                       in1=nbias[:, (u % NQ) * HQ + h], scale=1.0, scalar=BIG,
                                                       op0=ALU.add, op1=ALU.min, accum_out=nmax[:, u % NB, h:h + 1])
                i.then_inc(sb_ready, 1)

            def copy_pt(b, u, early):
                dve.wait_ge(pt_psum, b * UNITS + (u + 1))
                if not early:
                    dve.wait_ge(pv_done, b * UNITS + (u - 1))
                nc.vector.tensor_copy(pt_s[:, u % 2], bank[2 + u % 2][:]).then_inc(pt_ready, 1)

            def inverse(b, par, n, early=False):
                dve.wait_ge(p_ready, b * UNITS + (n + 1) * NQ)
                nc.vector.reciprocal(rinv, rsum[:, (par + n) % 2]).then_inc(rinv_ready, 1)
                dve.wait_ge(rinv_ready, b * NWIN + (n + 1))
                if not early:
                    dve.wait_ge(rb_done, b * NWIN + n)
                nc.vector.tensor_scalar(rexp[:], bc(rinv, 2, [P, H, HD]), inv_count[:, n:n + 1], None,
                                        ALU.mult).then_inc(rexp_ready, 1)

            def weigh(b, par, n, early=False):
                dve.wait_ge(rb_done, b * NWIN + (n + 1))
                dve.wait_ge(vsum_ready, b * NWIN + (n + 1))
                if not early:
                    dve.wait_ge(acc_done, b * NWIN + (n - 1))
                nc.vector.tensor_tensor(ct[:, (par + n) % 2], bank[4 + (par + n) % 2][:, DC * W:2 * DC * W].rearrange("p (c k) -> p c k", c=DC),
                                        vsum.rearrange("p (c k) -> p c k", c=DC), ALU.mult).then_inc(ct_ready, 1)

            def add_residual(b, t):
                dve.wait_ge(res_biased, b + 1)
                dve.wait_ge(o_done, b * TB + (t + 1) + OPEN)
                nc.vector.tensor_tensor(stage[:, t, 0:D], bank[6 + t % 2][:, 0:D], stage[:, t, 0:D],
                                        ALU.add).then_inc(res_ready, 1)

            def batch(b, par, first_, last):
                step = None
                for u in range(UNITS):
                    if ahead(b, u, last):
                        b2, u2 = ahead(b, u, last)
                        biased(b2, u2, first_ and 2 <= u2 < NB)
                    copy_pt(b, u, first_ and u < 2)
                    n = u // NQ - 1
                    if u % NQ == 0:
                        if n >= 0:
                            inverse(b, par, n, first_ and n == 0)
                        elif not first_:
                            inverse(b - 1, 1 - par, NWIN - 1)
                    if u % NQ == 3:
                        if n >= 0:
                            weigh(b, par, n, first_ and n < 2)
                        elif not first_:
                            weigh(b - 1, 1 - par, NWIN - 1)
                    for s in steps(u, first_, last):
                        if s == "stats0":
                            dve.wait_ge(xb_loaded, (b + 2) * 16)
                            norm = norm_stats(prep_use(b + 1), xb, mean_b[:])
                            next(norm)
                        if s == "r_stats0":
                            dve.wait_ge(res_ready, b * TB + OPEN)
                            r_norm = stats_route(route_use(b - 1), stage, stage_i, (b - 1) * TB)
                            next(r_norm)
                        if s == "stats1":
                            next(norm, None)
                        if s == "r_stats1":
                            next(r_norm, None)
                        if s in ("norm0", "norm1"):
                            normalise(prep_use(b + 1), xb, mean_b[:], ln_t[:, 4, :], int(s[-1]))
                        if s in ("r_norm0", "r_norm1"):
                            norm_route(route_use(b - 1), stage, int(s[-1]))
                        if s in ("copy_v0", "copy_v1", "copy_v2", "copy_v3"):
                            copy_v(b + 1, 1 - par, int(s[-1]))
                        if s in ("add0", "add1", "add2", "add3"):
                            add_residual(b - 1, int(s[-1]))
                        if s == "choose0":
                            parts = choose(b + (B - 1), stage)
                        if s in ("choose0", "choose1", "choose2", "choose3"):
                            step = next(parts)
                        if s == "place":
                            find_place(b + (B - 1), B, bank[7], step)

            for t in range(TB):
                copy_v(0, 0, t)
            biased(0, 0, True)
            biased(0, 1, True)
            two_by_two(dve, batch)
            inverse(B - 1, 1, NWIN - 1)
            weigh(B - 1, 1, NWIN - 1)
            for t in range(TB):
                add_residual(B - 1, t)
            dve.wait_ge(res_ready, B * TB + OPEN)
            whole(stats_route(route_use(B - 1), stage, stage_i, (B - 1) * TB))
            norm_route(route_use(B - 1), stage)
            step = whole(choose(2 * B - 1, stage))
            find_place(2 * B - 1, B, bank[6], step)
            tables(1, bank[7])
            ffn(1)


_INS = ['L0_attn_hidden_states', 'L0_attn_Wq', 'L0_attn_bq', 'L0_attn_Wk', 'L0_attn_bk', 'L0_attn_Wv', 'L0_attn_bv',
        'L0_attn_Wo', 'L0_attn_bo', 'L0_attn_pos_bias', 'L0_ffn_macro_w', 'L0_ffn_micro_w', 'L0_ffn_gate_w',
        'L0_ffn_up_w', 'L0_ffn_down_w']


def kernel(**inputs):
    import numpy as _np
    import concourse.bacc as _bacc
    from concourse import mybir as _mybir
    from concourse.bass_utils import run_bass_kernel_spmd as _run

    nc = _bacc.Bacc("TRN2", target_bir_lowering=False, num_devices=1)
    arrays, args = {}, []
    for name in _INS:
        a = _np.ascontiguousarray(inputs[name])
        arrays[f"in_{name}"] = a
        args.append(nc.dram_tensor(f"in_{name}", a.shape, _mybir.dt.from_np(a.dtype), kind="ExternalInput").ap())
    args.append(nc.dram_tensor("out_0", (T + (G + 1) * P, D), F32, kind="ExternalOutput").ap())
    macaron_kernel(nc, *args)
    r = _run(nc, [arrays], core_ids=[0])
    return r.results[0]["out_0"][:T].reshape(B, S, D)
```
